# Optimizing a Trainium2 kernel written in Bass

```python
import numpy as np
import jax
import jax.numpy as jnp

def _softmax(x, axis=-1):
    return jax.nn.softmax(x, axis=axis)

def _gelu(x):
    return jax.nn.gelu(x, approximate=True)

def _silu(x):
    return jax.nn.silu(x)

def _sigmoid(x):
    return jax.nn.sigmoid(x)

def _layernorm(x, axis=-1, eps=1e-05):
    m = jnp.mean(x, axis=axis, keepdims=True)
    v = jnp.var(x, axis=axis, keepdims=True)
    return (x - m) / jnp.sqrt(v + eps)

def _scatter_add(tgt, idx, src, axis=0):
    return tgt.at[idx].add(src)

def _segment_sum(src, seg, n):
    return jax.ops.segment_sum(src, seg, n)
kernel_name = 'mk_gnn_preln_d2_gnn_r32_dab336'

def setup_inputs(seed: int=0):
    np.random.seed(seed)
    _w = jnp.asarray

    def _rec_inputs():
        import jax
        import jax.numpy as jnp
        _gk = jax.random.key(seed)
        x = -0.0002928 + 1 * jax.random.normal(jax.random.fold_in(_gk, 1), (50000, 64), jnp.float32)
        src = jax.random.randint(jax.random.fold_in(_gk, 2), (50000,), 0, 50000, jnp.int32)
        dst = jnp.minimum((50000 * jax.random.uniform(jax.random.fold_in(_gk, 3), (50000,)) ** 2.0).astype(jnp.int32), 49999)
        _o = jnp.argsort(dst, stable=True)
        src = src[_o]
        dst = dst[_o]
        edge_weight = jax.random.uniform(jax.random.fold_in(_gk, 13), (50000,), jnp.float32, 0.0, 0.999999)
        edge_weight_n2 = jax.random.uniform(jax.random.fold_in(_gk, 14), (50000,), jnp.float32, 0.0, 0.999999)
        return (x, src, dst, edge_weight, edge_weight_n2)
    x, src, dst, edge_weight, edge_weight_n2 = _rec_inputs()

    def _L0_gnn_setup():
        import jax, jax.numpy as jnp
        import numpy as np
        N, E, D_IN, D_OUT = (2048, 32768, 64, 64)
        EPS = 1e-08
        key = jax.random.key(seed)
        ks = jax.random.split(key, 8)
        h = jax.random.normal(ks[0], (N, D_IN), dtype=jnp.float32)
        edge_index = jax.random.randint(ks[1], (2, E), 0, N, dtype=jnp.int64 if jax.config.jax_enable_x64 else jnp.int32)
        adj_v = jax.random.uniform(ks[2], (E,), dtype=jnp.float32)
        deg_v = jax.random.uniform(ks[3], (E,), dtype=jnp.float32)
        W = jax.random.normal(ks[4], (D_IN, D_OUT), dtype=jnp.float32) / np.sqrt(D_IN)
        b = jax.random.normal(ks[5], (D_OUT,), dtype=jnp.float32) * 0.01
        deg_coeff = jnp.array([0.5, 0.0], dtype=jnp.float32)
        coeff_param = jnp.zeros((3,), dtype=jnp.float32)
        scale_param = 2.0 * jnp.ones((1,), dtype=jnp.float32)
        return {'h': h, 'edge_index': edge_index, 'adj_v': adj_v, 'deg_v': deg_v, 'W': W, 'b': b, 'deg_coeff': deg_coeff, 'coeff_param': coeff_param, 'scale_param': scale_param}
    _L0_gnn_all = _L0_gnn_setup()
    _L0_gnn_in = {k: v for k, v in _L0_gnn_all.items() if k in ('W', 'b', 'deg_coeff', 'coeff_param', 'scale_param')}
    del _L0_gnn_all

    def _L1_gnn_setup():
        import jax, jax.numpy as jnp
        import numpy as np
        N_NODES = 50000
        N_EDGES = 25000
        D_IN = 64
        D_MSG = 64
        D_UP = 64
        D_H = 128

        def _mlp(x, W1, b1, W2, b2):
            return jax.nn.relu(x @ W1 + b1) @ W2 + b2
        key = jax.random.key(seed)
        ks = jax.random.split(key, 12)

        def glorot(k, shape):
            lim = np.sqrt(6.0 / (shape[0] + shape[1]))
            return jax.random.uniform(k, shape, jnp.float32, -lim, lim)
        x = jax.random.normal(ks[0], (N_NODES, D_IN), jnp.float32)
        edge_index = jax.random.randint(ks[1], (2, N_EDGES), 0, N_NODES, jnp.int32)
        degrees = jax.random.uniform(ks[2], (N_NODES,), jnp.float32)
        mW1 = glorot(ks[3], (2 * D_IN, D_H))
        mb1 = jnp.zeros((D_H,), jnp.float32)
        mW2 = glorot(ks[4], (D_H, D_MSG))
        mb2 = jnp.zeros((D_MSG,), jnp.float32)
        uW1 = glorot(ks[5], (D_IN + D_MSG, D_H))
        ub1 = jnp.zeros((D_H,), jnp.float32)
        uW2 = glorot(ks[6], (D_H, D_UP))
        ub2 = jnp.zeros((D_UP,), jnp.float32)
        return {'x': x, 'edge_index': edge_index, 'degrees': degrees, 'mW1': mW1, 'mb1': mb1, 'mW2': mW2, 'mb2': mb2, 'uW1': uW1, 'ub1': ub1, 'uW2': uW2, 'ub2': ub2}
    _L1_gnn_all = _L1_gnn_setup()
    _L1_gnn_in = {k: v for k, v in _L1_gnn_all.items() if k in ('mW1', 'mb1', 'mW2', 'mb2', 'uW1', 'ub1', 'uW2', 'ub2')}
    del _L1_gnn_all
    return {'x': x, 'src': src, 'dst': dst, 'edge_weight': edge_weight, 'edge_weight_n2': edge_weight_n2, 'L0_gnn_W': _L0_gnn_in['W'], 'L0_gnn_b': _L0_gnn_in['b'], 'L0_gnn_deg_coeff': _L0_gnn_in['deg_coeff'], 'L0_gnn_coeff_param': _L0_gnn_in['coeff_param'], 'L0_gnn_scale_param': _L0_gnn_in['scale_param'], 'L1_gnn_mW1': _L1_gnn_in['mW1'], 'L1_gnn_mb1': _L1_gnn_in['mb1'], 'L1_gnn_mW2': _L1_gnn_in['mW2'], 'L1_gnn_mb2': _L1_gnn_in['mb2'], 'L1_gnn_uW1': _L1_gnn_in['uW1'], 'L1_gnn_ub1': _L1_gnn_in['ub1'], 'L1_gnn_uW2': _L1_gnn_in['uW2'], 'L1_gnn_ub2': _L1_gnn_in['ub2']}

def reference(x, src, dst, edge_weight, edge_weight_n2, L0_gnn_W, L0_gnn_b, L0_gnn_deg_coeff, L0_gnn_coeff_param, L0_gnn_scale_param, L1_gnn_mW1, L1_gnn_mb1, L1_gnn_mW2, L1_gnn_mb2, L1_gnn_uW1, L1_gnn_ub1, L1_gnn_uW2, L1_gnn_ub2):
    import jax
    import jax.numpy as jnp

    def _L0_gnn_ref(h, edge_index, adj_v, deg_v, W, b, deg_coeff, coeff_param, scale_param):
        import jax, jax.numpy as jnp
        import numpy as np
        N, E, D_IN, D_OUT = (2048, 32768, 64, 64)
        EPS = 1e-08
        n_nodes = h.shape[0]
        Wh = h @ W + b
        row, col = (edge_index[0], edge_index[1])
        sc = jax.nn.softplus(deg_coeff[0] * deg_v + deg_coeff[1])
        Wr = Wh[row]
        Wc = Wh[col]
        dot = jnp.sum(Wr * Wc, axis=-1)
        nr = jnp.sqrt(jnp.sum(Wr * Wr, axis=-1))
        nc = jnp.sqrt(jnp.sum(Wc * Wc, axis=-1))
        sim = dot / jnp.maximum(nr * nc, EPS)
        sim_pos = jax.nn.relu(sim)
        sim_neg = -jax.nn.relu(-sim)
        no_diag = (row != col).astype(Wh.dtype)
        base = adj_v * sc * no_diag
        prop_pos = jax.ops.segment_sum((base * sim_pos)[:, None] * Wc, row, num_segments=n_nodes)
        prop_neg = jax.ops.segment_sum((base * sim_neg)[:, None] * Wc, row, num_segments=n_nodes)
        coeff = jax.nn.softmax(coeff_param)
        scale = jax.nn.softplus(scale_param)
        return scale * (coeff[0] * prop_pos + coeff[1] * prop_neg + coeff[2] * Wh)

    def _L1_gnn_ref(x, edge_index, degrees, mW1, mb1, mW2, mb2, uW1, ub1, uW2, ub2):
        import jax, jax.numpy as jnp
        import numpy as np
        N_NODES = 50000
        N_EDGES = 25000
        D_IN = 64
        D_MSG = 64
        D_UP = 64
        D_H = 128

        def _mlp(x, W1, b1, W2, b2):
            return jax.nn.relu(x @ W1 + b1) @ W2 + b2
        idx_i = edge_index[1]
        idx_j = edge_index[0]
        x_i = x[idx_i]
        x_j = x[idx_j]
        msgs = _mlp(jnp.concatenate([x_i, x_j], axis=-1), mW1, mb1, mW2, mb2)
        agg = jax.ops.segment_sum(msgs, idx_i, num_segments=x.shape[0])
        out = _mlp(jnp.concatenate([x, agg], axis=-1), uW1, ub1, uW2, ub2)
        return out
    edge_index = jnp.stack([src, dst])
    deg = jnp.maximum(jax.ops.segment_sum(jnp.ones(dst.shape, jnp.float32), dst, num_segments=50000), 1.0)
    deg_isqrt = deg ** (-0.5)
    h = jnp.maximum(_layernorm(x, axis=-1), 0.0)
    x = x + _L0_gnn_ref(h, edge_index, edge_weight, edge_weight_n2, L0_gnn_W, L0_gnn_b, L0_gnn_deg_coeff, L0_gnn_coeff_param, L0_gnn_scale_param)
    h = jnp.maximum(_layernorm(x, axis=-1), 0.0)
    x = x + _L1_gnn_ref(h, edge_index, deg_isqrt, L1_gnn_mW1, L1_gnn_mb1, L1_gnn_mW2, L1_gnn_mb2, L1_gnn_uW1, L1_gnn_ub1, L1_gnn_uW2, L1_gnn_ub2)
    return x

_drawn_inputs = setup_inputs


def setup_inputs(seed=0):
    import zlib

    import numpy as np

    out = dict(_drawn_inputs(seed))
    spreads = {'L0_gnn_coeff_param': (0.0, 0.1),
     'L1_gnn_mb1': (0.0, 0.1),
     'L1_gnn_mb2': (0.0, 0.1),
     'L1_gnn_ub1': (0.0, 0.1),
     'L1_gnn_ub2': (0.0, 0.1)}
    factors = {'edge_weight_n2': 8.0, 'L0_gnn_b': 6.452, 'L0_gnn_deg_coeff': 5.971}
    for name, (base, spread) in spreads.items():
        noise = np.random.default_rng([zlib.crc32(name.encode()), seed]).standard_normal(out[name].shape)
        drawn = base * np.exp(spread * noise) if base else spread * noise
        out[name] = jnp.asarray(drawn.astype(out[name].dtype))
    for name, factor in factors.items():
        out[name] = (out[name] * factor).astype(out[name].dtype)
    return out
```

```python
import concourse.bass as bass
from concourse import mybir
from contextlib import ExitStack

FP32 = mybir.dt.float32
INT32 = mybir.dt.int32
ALU = mybir.AluOpType
ACT = mybir.ActivationFunctionType
AX = mybir.AxisListType

P = 128
N = 50000
E = 50000
D = 64
DH = 128
R = 8
BLOCK = P * R
BLOCKS = -(-N // BLOCK)
LAST_BASE = N - BLOCK
PAIRS = BLOCKS // 2
G = 4
TILES = 392
GROUPS = TILES // G
GPAIRS = GROUPS // 2
ROWS = N + P
CHUNKS = -(-TILES // P)
FULL = CHUNKS - 1
LAST_T = TILES - FULL * P
REST = E - FULL * P * P
REST_T, REST_E = REST // P, REST % P
EPS_LN = 1e-5
EPS_SIM = 1e-8

assert BLOCKS % 2 == 1 and GROUPS % 2 == 0 and TILES * P >= E and REST_E > 0


class Steps:

    def __init__(self, eng, sem, start=0):
        self.eng, self.sem, self.n, self.made = eng, sem, start, 0

    def mark(self, ins):
        self.n = self.n + 1
        self.made += 1
        ins.then_inc(self.sem, 1)

    def wait(self):
        self.eng.wait_ge(self.sem, self.n)

    def link(self, ins):
        self.mark(ins)
        self.wait()


def began(k):
    return not isinstance(k, int) or k > 0


def rounds(eng, n, first=0):
    yield first
    with eng.Fori(first + 1, n) as k:
        yield k


def rows_of(tab, base, r=R):
    return tab[bass.ds(base, P * r), :].rearrange("(p r) d -> p (r d)", r=r)


def build(nc, x, src, dst, edge_weight, edge_weight_n2, W, b, deg_coeff, coeff_param, scale_param,
          mW1, mb1, mW2, mb2, uW1, ub1, uW2, ub2, out):
    ctx = ExitStack()
    with ctx:
        def sb(name, shape, dt=FP32):
            return ctx.enter_context(nc.sbuf_tensor(name, shape, dt))

        def table(name, shape):
            return nc.dram_tensor(name, shape, FP32, kind="Internal").ap()

        tabs = {name: table(name, [ROWS, D]) for name in ("wh", "x1")}
        tabs["h1_agg"] = table("h1_agg", [2 * ROWS, D])
        tabs["ends"] = table("ends", [2, TILES, P])

        c = dict(
            ident=sb("ident", [P, P]),
            upper=sb("upper", [P, P]),
            zeros=sb("zeros", [P, R * D]),
            eps_ln=sb("eps_ln", [P, 1]),
            trash=sb("trash", [P, G]),
            w_blk=sb("w_blk", [P, 2 * D]),
            b_row=sb("b_row", [P, D]),
            mw1=sb("mw1", [P, DH]), mb1_col=sb("mb1_col", [P, 1]),
            mw2=sb("mw2", [P, D]), mb2_row=sb("mb2_row", [P, D]),
            uw1=sb("uw1", [P, DH]), ub1_col=sb("ub1_col", [P, 1]),
            uw2=sb("uw2", [P, D]), ub2_row=sb("ub2_row", [P, D]),
            mix=sb("mix", [P, 3]),
            edge_f=sb("edge_f", [P, 3, GROUPS + 2, G]),
            edge_i=[sb(f"edge_i{layer}", [P, 2, GROUPS + 2, G], INT32) for layer in range(2)],
            bank=[ctx.enter_context(nc.psum_tensor(f"bank{i}", [P, 512], FP32)) for i in range(8)],
        )
        prepare(nc, c, tabs, src, dst, edge_weight, edge_weight_n2, W, b, deg_coeff, coeff_param,
                scale_param, mW1, mb1, mW2, mb2, uW1, ub1, uW2, ub2)
        node_phase0(nc, c, tabs, x)
        edge_phase(nc, c, tabs, layer=0)
        node_phase1(nc, c, tabs)
        edge_phase(nc, c, tabs, layer=1)
        node_phase2(nc, c, tabs, out)


def prepare(nc, c, tabs, src, dst, edge_weight, edge_weight_n2, W, b, deg_coeff, coeff_param,
            scale_param, mW1, mb1, mW2, mb2, uW1, ub1, uW2, ub2):
    with ExitStack() as ctx:
        def sb(name, shape, dt=FP32):
            return ctx.enter_context(nc.sbuf_tensor(name, shape, dt))

        def sem(name):
            return ctx.enter_context(nc.semaphore(name))

        rows_i = sb("rows_i", [P, 2, CHUNKS, P], INT32)
        rows_f = sb("rows_f", [P, 4, CHUNKS, P])
        trash_i = sb("trash_i", [P, G], INT32)
        TC = GROUPS * G
        adj = sb("adj", [P, TC])
        deg = sb("deg", [P, TC + 1])
        soft = [sb(f"soft{i}", [P, TC + 1]) for i in range(3)]
        differ = sb("differ", [P, TC])
        dc = sb("dc", [P, 2])
        cp = sb("cp", [P, 3])
        cps = [sb(f"cps{i}", [P, 3]) for i in range(4)]

        pads_made, rows_loaded, consts_loaded = sem("pads_made"), sem("rows_loaded"), sem("consts_loaded")
        pool_steps, pool_made, dve_steps = sem("pool_steps"), sem("pool_made"), sem("dve_steps")
        rows_ready, cols_done, soft_in, soft_exp, mix_in, mix_exp = (
            sem("rows_ready"), sem("cols_done"), sem("soft_in"), sem("soft_exp"), sem("mix_in"),
            sem("mix_exp"))
        soft_log, cols_taken, ends_stored, blk_clear = (
            sem("soft_log"), sem("cols_taken"), sem("ends_stored"), sem("blk_clear"))

        with nc.Block() as block:
            @block.sync
            def _(sp):
                sp.wait_ge(pads_made, 4)
                n = 0
                for i, (rows, arr) in enumerate(((rows_i[:, 0], src), (rows_i[:, 1], dst),
                                                 (rows_f[:, 2], edge_weight),
                                                 (rows_f[:, 3], edge_weight_n2))):
                    whole = FULL * P * P
                    sp.dma_start(rows[:, 0:FULL, :],
                                 arr[0:whole].rearrange("(c q e) -> q c e", q=P, e=P)).then_inc(rows_loaded, 16)
                    sp.dma_start(rows[0:REST_T, FULL, :],
                                 arr[whole:whole + REST_T * P].rearrange("(q e) -> q e", e=P)).then_inc(rows_loaded, 16)
                    sp.dma_start(rows[REST_T:REST_T + 1, FULL, 0:REST_E],
                                 arr[whole + REST_T * P:E].rearrange("(q e) -> q e", q=1)).then_inc(rows_loaded, 16)
                sp.wait_ge(rows_ready, 1)
                for i in range(2):
                    sp.dma_start(tabs["ends"][i, 0:FULL * P, :].rearrange("(c q) e -> q c e", q=P),
                                 rows_f[:, i, 0:FULL, :]).then_inc(ends_stored, 16)
                    sp.dma_start(tabs["ends"][i, FULL * P:TILES, :],
                                 rows_f[0:LAST_T, i, FULL, :]).then_inc(ends_stored, 16)
                sp.wait_ge(ends_stored, 64)

            @block.scalar
            def _(act):
                act.wait_ge(blk_clear, 1)
                row = lambda v: v.rearrange("(a n) -> a n", a=1)
                col = lambda v: v.rearrange("(n a) -> n a", a=1)
                loads = [(c["w_blk"][0:D, 0:D], W), (c["w_blk"][D:2 * D, D:2 * D], W),
                         (c["mw1"][:], mW1), (c["mw2"][:], mW2), (c["uw1"][:], uW1), (c["uw2"][:], uW2),
                         (c["mb1_col"][:], col(mb1)), (c["ub1_col"][:], col(ub1)),
                         (c["b_row"][:], row(b).to_broadcast([P, D])),
                         (c["mb2_row"][:], row(mb2).to_broadcast([P, D])),
                         (c["ub2_row"][:], row(ub2).to_broadcast([P, D])),
                         (dc[:], row(deg_coeff).to_broadcast([P, 2])),
                         (cp[:], row(coeff_param).to_broadcast([P, 3])),
                         (deg[:, TC:TC + 1], row(scale_param).to_broadcast([P, 1]))]
                with nc.allow_non_contiguous_dma(reason="bias columns"):
                    for to, of in loads:
                        act.dma_start(to, of).then_inc(consts_loaded, 16)
                act.wait_ge(soft_in, 1)
                nc.scalar.activation(soft[1][:], soft[2][:], ACT.Exp, scale=-1.0).then_inc(soft_exp, 1)
                act.wait_ge(mix_in, 1)
                nc.scalar.activation(cps[1][:], cps[0][:], ACT.Exp).then_inc(mix_exp, 1)
                act.wait_ge(soft_exp, 1)
                nc.scalar.activation(soft[2][:], soft[1][:], ACT.Ln, bias=1.0).then_inc(soft_log, 1)

            @block.gpsimd
            def _(pool):
                steps = Steps(pool, pool_steps)
                for i in range(2):
                    nc.gpsimd.iota(rows_i[0:LAST_T, i, FULL, :], pattern=[[1, P]], base=N,
                                   channel_multiplier=0).then_inc(pads_made, 1)
                for i in range(2):
                    nc.gpsimd.memset(rows_f[0:LAST_T, 2 + i, FULL, :], 0.0).then_inc(pads_made, 1)
                nc.gpsimd.memset(c["w_blk"][:], 0.0).then_inc(blk_clear, 1)
                steps.mark(nc.gpsimd.memset(c["ident"][:], 0.0))
                steps.mark(nc.gpsimd.memset(c["upper"][:], 1.0))
                steps.link(nc.gpsimd.iota(trash_i[:], pattern=[[0, G]], base=N, channel_multiplier=1))
                nc.gpsimd.affine_select(out=c["ident"][:], in_=c["ident"][:], compare_op=ALU.not_equal,
                                        fill=1.0, base=0, pattern=[[-1, P]],
                                        channel_multiplier=1).then_inc(pool_made, 1)
                nc.gpsimd.affine_select(out=c["upper"][:], in_=c["upper"][:], compare_op=ALU.is_ge,
                                        fill=0.0, base=0, pattern=[[1, P]],
                                        channel_multiplier=-1).then_inc(pool_made, 1)
                nc.gpsimd.tensor_copy(c["trash"][:], trash_i[:]).then_inc(pool_made, 1)
                nc.gpsimd.memset(c["zeros"][:], 0.0).then_inc(pool_made, 1)
                nc.gpsimd.memset(c["eps_ln"][:], EPS_LN).then_inc(pool_made, 1)
                for layer in range(2):
                    nc.gpsimd.memset(c["edge_i"][layer][:, :, GROUPS:GROUPS + 2, :], 0).then_inc(pool_made, 1)

            @block.tensor
            def _(pe):
                pe.wait_ge(pool_made, 1)
                pe.wait_ge(rows_ready, 1)
                for i in range(4):
                    for ch in range(CHUNKS):
                        q = P if ch < FULL else LAST_T
                        last = nc.tensor.transpose(c["bank"][i][:, ch * P:ch * P + q],
                                                   rows_f[0:q, i, ch, :], c["ident"][0:q, 0:q])
                    last.then_inc(cols_done, 1)

            @block.vector
            def _(dve):
                steps = Steps(dve, dve_steps)
                dve.wait_ge(rows_loaded, 12 * 16)
                for i in range(2):
                    steps.mark(nc.vector.tensor_copy(rows_f[:, i, 0:FULL, :], rows_i[:, i, 0:FULL, :]))
                steps.mark(nc.vector.tensor_copy(rows_f[0:LAST_T, 0, FULL, :], rows_i[0:LAST_T, 0, FULL, :]))
                nc.vector.tensor_copy(rows_f[0:LAST_T, 1, FULL, :],
                                      rows_i[0:LAST_T, 1, FULL, :]).then_inc(rows_ready, 1)
                dve.wait_ge(cols_done, 4)
                ef = c["edge_f"]
                flat = lambda a: a.rearrange("p g j -> p (g j)")
                for i in range(2):
                    steps.mark(nc.vector.tensor_copy(flat(ef[:, i, 0:GROUPS, :]), c["bank"][i][:, 0:TC]))
                    steps.mark(nc.vector.tensor_copy(flat(c["edge_i"][0][:, i, 0:GROUPS, :]), c["bank"][i][:, 0:TC]))
                    steps.mark(nc.vector.tensor_scalar(flat(c["edge_i"][1][:, i, 0:GROUPS, :]), c["bank"][i][:, 0:TC],
                                                       2.0, None, ALU.mult))
                steps.mark(nc.vector.tensor_copy(adj[:], c["bank"][2][:, 0:TC]))
                dve.wait_ge(consts_loaded, 14 * 16)
                steps.mark(nc.vector.tensor_scalar(soft[0][:, 0:TC], c["bank"][3][:, 0:TC], dc[:, 0:1], dc[:, 1:2],
                                                   ALU.mult, ALU.add))
                steps.link(nc.vector.tensor_copy(soft[0][:, TC:TC + 1], deg[:, TC:TC + 1]))
                nc.vector.scalar_tensor_tensor(soft[2][:], soft[0][:], -1.0, soft[0][:], ALU.mult, ALU.max).then_inc(soft_in, 1)
                steps.link(nc.vector.tensor_reduce(cps[3][:, 0:1], cp[:], AX.X, ALU.max))
                nc.vector.tensor_scalar(cps[0][:], cp[:], cps[3][:, 0:1], None, ALU.subtract).then_inc(mix_in, 1)
                steps.link(nc.vector.tensor_tensor(differ[:], flat(ef[:, 0, 0:GROUPS, :]),
                                                   flat(ef[:, 1, 0:GROUPS, :]), ALU.not_equal))
                steps.link(nc.vector.tensor_tensor(adj[:], adj[:], differ[:], ALU.mult))
                dve.wait_ge(mix_exp, 1)
                steps.link(nc.vector.tensor_reduce(cps[3][:, 1:2], cps[1][:], AX.X, ALU.add))
                steps.link(nc.vector.reciprocal(cps[3][:, 2:3], cps[3][:, 1:2]))
                steps.link(nc.vector.tensor_scalar(cps[2][:], cps[1][:], cps[3][:, 2:3], None, ALU.mult))
                dve.wait_ge(soft_log, 1)
                steps.link(nc.vector.scalar_tensor_tensor(soft[1][:], soft[0][:], 0.0, soft[2][:],
                                                          ALU.max, ALU.add))
                steps.mark(nc.vector.tensor_tensor(flat(ef[:, 2, 0:GROUPS, :]), adj[:], soft[1][:, 0:TC], ALU.mult))
                steps.link(nc.vector.tensor_scalar(c["mix"][:], cps[2][:], soft[1][:, TC:TC + 1], None, ALU.mult))


def layer_norm_front(nc, dve, steps, c, t, s, k):
    rows = lambda a: a.rearrange("p (r d) -> p r d", d=D)
    wide = lambda a: a[:, :].unsqueeze(2).to_broadcast([P, R, D])
    dve.wait_ge(t["x_loaded"][s], 16 * (k + 1))
    steps.link(nc.vector.tensor_reduce(t["total"][s][:], rows(t["x"][s][:]), AX.X, ALU.add))
    nc.vector.scalar_tensor_tensor(rows(t["xc"][s][:]), wide(t["total"][s]), -1.0 / D,
                                   rows(t["x"][s][:]), ALU.mult, ALU.add).then_inc(t["xc_ready"][s], 1)
    dve.wait_ge(t["sq_ready"][s], k + 1)
    nc.vector.tensor_reduce(t["ssq"][s][:], rows(t["sq"][s][:]), AX.X,
                            ALU.add).then_inc(t["ssq_ready"][s], 1)
    dve.wait_ge(t["std_ready"][s], k + 1)
    steps.link(nc.vector.reciprocal(t["rstd"][s][:], t["std"][s][:]))
    if began(k):
        dve.wait_ge(t["h_free"][s], t["h_per"] * k)
    nc.vector.scalar_tensor_tensor(t["h_rows"][s], rows(t["xc"][s][:]), 0.0, wide(t["rstd"][s]),
                                   ALU.max, ALU.mult).then_inc(t["h_ready"][s], 1)


def layer_norm_act(nc, act, c, t, s, k):
    act.wait_ge(t["xc_ready"][s], k + 1)
    nc.scalar.activation(t["sq"][s][:], t["xc"][s][:], ACT.Square).then_inc(t["sq_ready"][s], 1)
    act.wait_ge(t["ssq_ready"][s], k + 1)
    nc.scalar.activation(t["std"][s][:], t["ssq"][s][:], ACT.Sqrt, bias=c["eps_ln"][:, 0:1],
                         scale=1.0 / D).then_inc(t["std_ready"][s], 1)


def norm_buffers(ctx, nc, tag):
    def two(name, shape):
        return [ctx.enter_context(nc.sbuf_tensor(f"{tag}_{name}{s}", shape, FP32)) for s in range(2)]

    def pair(name):
        return [ctx.enter_context(nc.semaphore(f"{tag}_{name}{s}")) for s in range(2)]

    t = {name: two(name, [P, R * D]) for name in ("x", "xc", "sq")}
    t |= {name: two(name, [P, R]) for name in ("total", "ssq", "std", "rstd")}
    t |= {name: pair(name) for name in ("x_loaded", "xc_ready", "sq_ready", "ssq_ready", "std_ready",
                                        "h_ready")}
    return t, two, pair


def node_phase0(nc, c, tabs, x):
    with ExitStack() as ctx:
        t, two, pair = norm_buffers(ctx, nc, "n0")
        hT, wh, x1 = two("hT", [P, 512]), two("wh", [P, R * D]), two("x1", [P, R * D])
        turned, hT_ready, wh_done, x1_ready = (pair(n) for n in ("turned", "hT_ready", "wh_done", "x1_ready"))
        stored = pair("stored")
        steps_sem = ctx.enter_context(nc.semaphore("n0_steps"))
        pads_stored = ctx.enter_context(nc.semaphore("n0_pads_stored"))
        h = two("h", [P, R * D])
        t["h_rows"] = [a[:].rearrange("p (r d) -> p r d", d=D) for a in h]
        t["h_free"], t["h_per"] = turned, 1
        bank = c["bank"]
        block = ctx.enter_context(nc.Block())

        @block.sync
        def _(sp):
            def load(s, k, base):
                if began(k):
                    sp.wait_ge(x1_ready[s], k)
                sp.dma_start(t["x"][s][:], rows_of(x, base)).then_inc(t["x_loaded"][s], 16)

            for k in rounds(sp, PAIRS):
                for s in range(2):
                    load(s, k, (2 * k + s) * BLOCK)
            load(0, PAIRS, LAST_BASE)

        @block.vector
        def _(dve):
            FRONT, BACK = 2, 1
            wide = lambda a: a[:, :].unsqueeze(1).to_broadcast([P, R, D])
            rows = lambda a: a.rearrange("p (r d) -> p r d", d=D)

            def front(s, k, steps):
                layer_norm_front(nc, dve, steps, c, t, s, k)

            def back(s, k, steps):
                dve.wait_ge(wh_done[s], k + 1)
                if began(k):
                    dve.wait_ge(stored[s], 32 * k)
                steps.link(nc.vector.tensor_tensor(rows(wh[s][:]), rows(bank[2 + s][:]), wide(c["b_row"]), ALU.add))
                nc.vector.scalar_tensor_tensor(x1[s][:], wh[s][:], c["mix"][:, 2:3], t["x"][s][:],
                                               ALU.mult, ALU.add).then_inc(x1_ready[s], 1)

            front(0, 0, Steps(dve, steps_sem))
            per = 2 * (FRONT + BACK)
            for k in rounds(dve, PAIRS):
                steps = Steps(dve, steps_sem, k * per + FRONT)
                front(1, k, steps)
                back(0, k, steps)
                front(0, k + 1, steps)
                back(1, k, steps)
                assert steps.made == per
            back(0, PAIRS, Steps(dve, steps_sem, PAIRS * per + FRONT))

        @block.scalar
        def _(act):
            def unit(s, k):
                layer_norm_act(nc, act, c, t, s, k)
                act.wait_ge(turned[s], k + 1)
                nc.scalar.copy(hT[s][:], bank[s][:]).then_inc(hT_ready[s], 1)

            for k in rounds(act, PAIRS):
                for s in range(2):
                    unit(s, k)
            unit(0, PAIRS)

        @block.tensor
        def _(pe):
            def unit(s, k):
                pe.wait_ge(t["h_ready"][s], k + 1)
                if began(k):
                    pe.wait_ge(hT_ready[s], k)
                for q in range(R // 2):
                    last = nc.tensor.transpose(bank[s][:, q * P:(q + 1) * P],
                                               h[s][:, q * 2 * D:(q + 1) * 2 * D], c["ident"][:])
                last.then_inc(turned[s], 1)
                pe.wait_ge(hT_ready[s], k + 1)
                if began(k):
                    pe.wait_ge(x1_ready[s], k)
                for q in range(R // 2):
                    last = nc.tensor.matmul(bank[2 + s][:, q * P:(q + 1) * P], hT[s][:, q * P:(q + 1) * P],
                                            c["w_blk"][:], start=True, stop=True)
                last.then_inc(wh_done[s], 1)

            for k in rounds(pe, PAIRS):
                for s in range(2):
                    unit(s, k)
            unit(0, PAIRS)

        @block.gpsimd
        def _(pool):
            for name in ("wh", "x1"):
                pool.dma_start(tabs[name][N:ROWS, :], c["zeros"][:, 0:D]).then_inc(pads_stored, 16)
            pool.dma_start(rows_of(tabs["h1_agg"], 2 * N, 2), c["zeros"][:, 0:2 * D]).then_inc(pads_stored, 16)

            def store(s, k, base):
                pool.wait_ge(x1_ready[s], k + 1)
                pool.dma_start(rows_of(tabs["wh"], base), wh[s][:]).then_inc(stored[s], 16)
                pool.dma_start(rows_of(tabs["x1"], base), x1[s][:]).then_inc(stored[s], 16)

            for k in rounds(pool, PAIRS):
                for s in range(2):
                    store(s, k, (2 * k + s) * BLOCK)
            pool.wait_ge(stored[1], 32 * PAIRS)
            store(0, PAIRS, LAST_BASE)
            pool.wait_ge(stored[0], 32 * (PAIRS + 1))
            pool.wait_ge(pads_stored, 48)


def node_phase1(nc, c, tabs):
    with ExitStack() as ctx:
        t, two, pair = norm_buffers(ctx, nc, "n1")
        stored = pair("stored")
        h_agg = two("h_agg", [P, R, 2, D])
        t["h_rows"] = [a[:, :, 0, :] for a in h_agg]
        steps_sem = ctx.enter_context(nc.semaphore("n1_steps"))
        halves_zero = ctx.enter_context(nc.semaphore("n1_halves_zero"))
        t["h_free"], t["h_per"] = stored, 16
        block = ctx.enter_context(nc.Block())

        @block.sync
        def _(sp):
            def load(s, k, base):
                if began(k):
                    sp.wait_ge(t["h_ready"][s], k)
                sp.dma_start(t["x"][s][:], rows_of(tabs["x1"], base)).then_inc(t["x_loaded"][s], 16)

            for k in rounds(sp, PAIRS):
                for s in range(2):
                    load(s, k, (2 * k + s) * BLOCK)
            load(0, PAIRS, LAST_BASE)

        @block.vector
        def _(dve):
            FRONT = 2
            for k in rounds(dve, PAIRS):
                steps = Steps(dve, steps_sem, k * 2 * FRONT)
                for s in range(2):
                    layer_norm_front(nc, dve, steps, c, t, s, k)
                assert steps.made == 2 * FRONT
            layer_norm_front(nc, dve, Steps(dve, steps_sem, PAIRS * 2 * FRONT), c, t, 0, PAIRS)

        @block.scalar
        def _(act):
            for k in rounds(act, PAIRS):
                for s in range(2):
                    layer_norm_act(nc, act, c, t, s, k)
            layer_norm_act(nc, act, c, t, 0, PAIRS)

        @block.gpsimd
        def _(pool):
            for s in range(2):
                nc.gpsimd.memset(h_agg[s][:, :, 1, :], 0.0).then_inc(halves_zero, 1)
            pool.wait_ge(halves_zero, 2)

            def store(s, k, base):
                pool.wait_ge(t["h_ready"][s], k + 1)
                pool.dma_start(rows_of(tabs["h1_agg"], 2 * base, 2 * R),
                               h_agg[s][:].rearrange("p r w d -> p (r w d)")).then_inc(stored[s], 16)

            for k in rounds(pool, PAIRS):
                for s in range(2):
                    store(s, k, (2 * k + s) * BLOCK)
            pool.wait_ge(stored[1], 16 * PAIRS)
            store(0, PAIRS, LAST_BASE)
            pool.wait_ge(stored[0], 16 * (PAIRS + 1))


def edge_phase(nc, c, tabs, layer):
    gathered = tabs["wh"] if layer == 0 else tabs["h1_agg"]
    added_to = tabs["x1"] if layer == 0 else tabs["h1_agg"]
    OWNER = layer
    L = f"e{layer}"
    with ExitStack() as ctx:
        def two(name, shape, dt=FP32):
            return [ctx.enter_context(nc.sbuf_tensor(f"{L}_{name}{s}", shape, dt)) for s in range(2)]

        def pair(name):
            return [ctx.enter_context(nc.semaphore(f"{L}_{name}{s}")) for s in range(2)]

        owners = two("owners", [P, G * P])
        ids = two("ids", [P, 2, G], INT32)
        ef = two("ef", [P, 3, G])
        ends = two("ends", [P, G, 2, D])
        same = two("same", [P, G, P])
        later = two("later", [P, G])
        to_trash = two("to_trash", [P, 3, G])
        to = two("to", [P, G], INT32)
        msgs = two("msgs", [P, G, D])
        sums = two("sums", [P, G, D])
        if layer == 0:
            prod, sq = two("prod", [P, G, D]), two("sq", [P, G, 2, D])
            dot, norm2, norm = two("dot", [P, G]), two("norm2", [P, G, 2]), two("norm", [P, G, 2])
            small = two("small", [P, 7, G])
        else:
            endsT, hid = two("endsT", [P, G * P]), two("hid", [P, G * P])
        owners_in, same_ready, ids_ready, gathers_in, to_ready, msgs_ready = (
            pair(n) for n in ("owners_in", "same_ready", "ids_ready", "gathers_in", "to_ready", "msgs_ready"))
        summed, sums_ready, added = (pair(n) for n in ("summed", "sums_ready", "added"))
        sq_ready, norm2_ready, norm_ready = (pair(n) for n in ("sq_ready", "norm2_ready", "norm_ready"))
        turned, endsT_ready, hid_done, hid_ready, mlp_done = (
            pair(n) for n in ("turned", "endsT_ready", "hid_done", "hid_ready", "mlp_done"))
        steps_sem = ctx.enter_context(nc.semaphore(f"{L}_steps"))
        waited = ctx.enter_context(nc.semaphore(f"{L}_waited"))
        bank = c["bank"]
        block = ctx.enter_context(nc.Block())

        @block.sync
        def _(sp):
            for k in rounds(sp, GPAIRS):
                for s in range(2):
                    if began(k):
                        sp.wait_ge(same_ready[s], k)
                    numbers = tabs["ends"][OWNER, bass.ds((2 * k + s) * G, G), :].rearrange("t e -> (t e)")
                    sp.dma_start(owners[s][:], numbers.partition_broadcast(P)).then_inc(owners_in[s], 16)

        @block.gpsimd
        def _(pool):
            def gathers(s, j):
                for w in range(2):
                    at = w if layer == 0 else 1 - w
                    pool.indirect_dma_start(
                        out=ends[s][:, j, at, :], out_offset=None, in_=gathered,
                        in_offset=bass.IndirectOffsetOnAxis(ap=ids[s][:, w, j:j + 1], axis=0),
                    ).then_inc(gathers_in[s], 16)

            def scatter(s, k, j):
                if j:
                    pool.wait_ge(added[s], 16 * G * k + 16 * j)
                elif s:
                    pool.wait_ge(added[0], 16 * G * (k + 1))
                elif began(k):
                    pool.wait_ge(added[1], 16 * G * k)
                pool.sem_inc(waited, 1)
                pool.indirect_dma_start(
                    out=added_to, out_offset=bass.IndirectOffsetOnAxis(ap=to[s][:, j:j + 1], axis=0),
                    in_=sums[s][:, j, :], in_offset=None, compute_op=ALU.add).then_inc(added[s], 16)

            for s in range(2):
                pool.wait_ge(ids_ready[s], 1)
                for j in range(G):
                    gathers(s, j)
            for k in rounds(pool, GPAIRS, 1):
                for s in range(2):
                    pool.wait_ge(ids_ready[s], k + 1)
                    pool.wait_ge(to_ready[s], k)
                    pool.wait_ge(sums_ready[s], k)
                    pool.sem_inc(waited, 1)
                    for j in range(G):
                        gathers(s, j)
                        scatter(s, k - 1, j)
            for s in range(2):
                pool.wait_ge(to_ready[s], GPAIRS)
                pool.wait_ge(sums_ready[s], GPAIRS)
                for j in range(G):
                    scatter(s, GPAIRS - 1, j)
            pool.wait_ge(added[1], 16 * G * GPAIRS)

        @block.vector
        def _(dve):
            for s in range(2):
                nc.vector.tensor_copy(ids[s][:], c["edge_i"][layer][:, :, s, :]).then_inc(ids_ready[s], 1)

            def unit(s, k, steps):
                group = 2 * k + s
                if began(k):
                    dve.wait_ge(to_ready[s], k)
                steps.link(nc.vector.tensor_copy(
                    ef[s][:], c["edge_f"][:, :, bass.ds(group, 1), :].rearrange("p w a j -> p w (a j)")))
                owner = ef[s][:, OWNER, :]
                dve.wait_ge(owners_in[s], 16 * (k + 1))
                if began(k):
                    dve.wait_ge(summed[s], k)
                for j in range(G):
                    last = nc.vector.scalar_tensor_tensor(
                        same[s][:, j, :], owners[s][:, j * P:(j + 1) * P], ef[s][:, OWNER, j:j + 1],
                        c["upper"][:], ALU.is_equal, ALU.mult, accum_out=later[s][:, j:j + 1])
                    if j < G - 1:
                        steps.mark(last)
                last.then_inc(same_ready[s], 1)
                steps.link(nc.vector.tensor_tensor(to_trash[s][:, 0, :], c["trash"][:], owner, ALU.subtract))
                dve.wait_ge(gathers_in[s], 2 * 16 * G * (k + 1))
                nc.vector.tensor_copy(
                    ids[s][:], c["edge_i"][layer][:, :, bass.ds(group + 2, 1), :].rearrange("p w a j -> p w (a j)"),
                ).then_inc(ids_ready[s], 1)
                if layer == 0:
                    a = small[s]
                    steps.link(nc.vector.tensor_tensor(prod[s][:], ends[s][:, :, 0, :], ends[s][:, :, 1, :], ALU.mult))
                    steps.mark(nc.vector.tensor_reduce(dot[s][:], prod[s][:], AX.X, ALU.add))
                    dve.wait_ge(sq_ready[s], k + 1)
                    nc.vector.tensor_reduce(norm2[s][:], sq[s][:], AX.X, ALU.add).then_inc(norm2_ready[s], 1)
                    dve.wait_ge(norm_ready[s], k + 1)
                    steps.link(nc.vector.tensor_tensor(a[:, 0, :], norm[s][:, :, 0], norm[s][:, :, 1], ALU.mult))
                    steps.link(nc.vector.tensor_scalar(a[:, 1, :], a[:, 0, :], EPS_SIM, None, ALU.max))
                    steps.link(nc.vector.reciprocal(a[:, 2, :], a[:, 1, :]))
                    steps.link(nc.vector.tensor_tensor(a[:, 3, :], dot[s][:], a[:, 2, :], ALU.mult))
                    steps.mark(nc.vector.tensor_scalar(a[:, 4, :], a[:, 3, :], 0.0, c["mix"][:, 0:1], ALU.max, ALU.mult))
                    steps.link(nc.vector.tensor_scalar(a[:, 5, :], a[:, 3, :], 0.0, c["mix"][:, 1:2], ALU.min, ALU.mult))
                    steps.link(nc.vector.tensor_tensor(a[:, 6, :], a[:, 4, :], a[:, 5, :], ALU.add))
                    steps.link(nc.vector.tensor_tensor(a[:, 0, :], a[:, 6, :], ef[s][:, 2, :], ALU.mult))
                    nc.vector.tensor_tensor(msgs[s][:], ends[s][:, :, 1, :],
                                            a[:, 0, :].unsqueeze(2).to_broadcast([P, G, D]),
                                            ALU.mult).then_inc(msgs_ready[s], 1)
                else:
                    dve.wait_ge(mlp_done[s], k + 1)
                    nc.vector.tensor_tensor(msgs[s][:], bank[4 + s][:, 0:G * D].rearrange("p (j d) -> p j d", d=D),
                                            c["mb2_row"][:, :].unsqueeze(1).to_broadcast([P, G, D]),
                                            ALU.add).then_inc(msgs_ready[s], 1)
                dve.wait_ge(same_ready[s], k + 1)
                steps.link(nc.vector.scalar_tensor_tensor(to_trash[s][:, 1, :], later[s][:], 1.5, to_trash[s][:, 0, :],
                                                          ALU.is_gt, ALU.mult))
                if began(k):
                    dve.wait_ge(added[s], 16 * G * k)
                if layer == 0:
                    nc.vector.tensor_tensor(to[s][:], to_trash[s][:, 1, :], owner, ALU.add).then_inc(to_ready[s], 1)
                else:
                    steps.link(nc.vector.tensor_tensor(to_trash[s][:, 2, :], to_trash[s][:, 1, :], owner, ALU.add))
                    nc.vector.tensor_scalar(to[s][:], to_trash[s][:, 2, :], 2.0, 1.0, ALU.mult,
                                            ALU.add).then_inc(to_ready[s], 1)

            per = 2 * (1 + (G - 1) + 1 + (10 if layer == 0 else 1) + 1)
            for k in rounds(dve, GPAIRS):
                steps = Steps(dve, steps_sem, k * per)
                for s in range(2):
                    unit(s, k, steps)
                assert steps.made == per, (steps.made, per)

        @block.scalar
        def _(act):
            def unit(s, k):
                if layer == 0:
                    act.wait_ge(gathers_in[s], 2 * 16 * G * (k + 1))
                    nc.scalar.activation(sq[s][:], ends[s][:], ACT.Square).then_inc(sq_ready[s], 1)
                    act.wait_ge(norm2_ready[s], k + 1)
                    nc.scalar.activation(norm[s][:], norm2[s][:], ACT.Sqrt).then_inc(norm_ready[s], 1)
                else:
                    act.wait_ge(turned[s], k + 1)
                    nc.scalar.copy(endsT[s][:], bank[s][:]).then_inc(endsT_ready[s], 1)
                    act.wait_ge(hid_done[s], k + 1)
                    nc.scalar.activation(hid[s][:], bank[2 + s][:], ACT.Relu,
                                         bias=c["mb1_col"][:, 0:1]).then_inc(hid_ready[s], 1)
                act.wait_ge(summed[s], k + 1)
                if began(k):
                    act.wait_ge(added[s], 16 * G * k)
                nc.scalar.copy(sums[s][:].rearrange("p j d -> p (j d)"),
                               bank[6 + s][:, 0:G * D]).then_inc(sums_ready[s], 1)

            for k in rounds(act, GPAIRS):
                for s in range(2):
                    unit(s, k)

        @block.tensor
        def _(pe):
            def unit(s, k):
                if layer == 1:
                    pe.wait_ge(gathers_in[s], 2 * 16 * G * (k + 1))
                    if began(k):
                        pe.wait_ge(endsT_ready[s], k)
                    for j in range(G):
                        last = nc.tensor.transpose(bank[s][:, j * P:(j + 1) * P],
                                                   ends[s][:, j].rearrange("p w d -> p (w d)"), c["ident"][:])
                    last.then_inc(turned[s], 1)
                    pe.wait_ge(endsT_ready[s], k + 1)
                    if began(k):
                        pe.wait_ge(hid_ready[s], k)
                    nc.tensor.matmul(bank[2 + s][:], c["mw1"][:], endsT[s][:], start=True,
                                     stop=True).then_inc(hid_done[s], 1)
                    pe.wait_ge(hid_ready[s], k + 1)
                    if began(k):
                        pe.wait_ge(msgs_ready[s], k)
                    for j in range(G):
                        last = nc.tensor.matmul(bank[4 + s][:, j * D:(j + 1) * D], hid[s][:, j * P:(j + 1) * P],
                                                c["mw2"][:], start=True, stop=True)
                    last.then_inc(mlp_done[s], 1)
                pe.wait_ge(same_ready[s], k + 1)
                pe.wait_ge(msgs_ready[s], k + 1)
                if began(k):
                    pe.wait_ge(sums_ready[s], k)
                for j in range(G):
                    last = nc.tensor.matmul(bank[6 + s][:, j * D:(j + 1) * D], same[s][:, j, :], msgs[s][:, j, :],
                                            start=True, stop=True)
                last.then_inc(summed[s], 1)

            for k in rounds(pe, GPAIRS):
                for s in range(2):
                    unit(s, k)


def node_phase2(nc, c, tabs, out):
    with ExitStack() as ctx:
        def two(name, shape):
            return [ctx.enter_context(nc.sbuf_tensor(f"n2_{name}{s}", shape, FP32)) for s in range(2)]

        def pair(name):
            return [ctx.enter_context(nc.semaphore(f"n2_{name}{s}")) for s in range(2)]

        H = BLOCK // 2
        x1, hs = two("x1", [P, R, D]), two("hs", [P, R, 2, D])
        hsT, hid, res = two("hsT", [P, BLOCK]), two("hid", [P, BLOCK]), two("res", [P, R, D])
        x1_in, hs_in, x1_biased, turned = (pair(n) for n in ("x1_in", "hs_in", "x1_biased", "turned"))
        hsT_low, hsT_high, hid_done, hid_ready, mlp_done, res_ready, stored = (
            pair(n) for n in ("hsT_low", "hsT_high", "hid_done", "hid_ready", "mlp_done", "res_ready", "stored"))
        bank = c["bank"]
        block = ctx.enter_context(nc.Block())

        @block.sync
        def _(sp):
            def load(s, k, base):
                if began(k):
                    sp.wait_ge(turned[s], k)
                sp.dma_start(hs[s][:].rearrange("p r w d -> p (r w d)"),
                             rows_of(tabs["h1_agg"], 2 * base, 2 * R)).then_inc(hs_in[s], 16)
                if began(k):
                    sp.wait_ge(res_ready[s], k)
                sp.dma_start(x1[s][:].rearrange("p r d -> p (r d)"),
                             rows_of(tabs["x1"], base)).then_inc(x1_in[s], 16)

            for k in rounds(sp, PAIRS):
                for s in range(2):
                    load(s, k, (2 * k + s) * BLOCK)
            load(0, PAIRS, LAST_BASE)

        @block.gpsimd
        def _(pool):
            def bias(s, k):
                pool.wait_ge(x1_in[s], 16 * (k + 1))
                nc.gpsimd.tensor_tensor(x1[s][:], x1[s][:], c["ub2_row"][:, :].unsqueeze(1).to_broadcast([P, R, D]),
                                        ALU.add).then_inc(x1_biased[s], 1)

            def store(s, k, base):
                pool.wait_ge(res_ready[s], k + 1)
                pool.dma_start(rows_of(out, base), res[s][:].rearrange("p r d -> p (r d)")).then_inc(stored[s], 16)

            bias(0, 0)
            for k in rounds(pool, PAIRS):
                bias(1, k)
                store(0, k, 2 * k * BLOCK)
                bias(0, k + 1)
                store(1, k, (2 * k + 1) * BLOCK)
            pool.wait_ge(stored[1], 16 * PAIRS)
            store(0, PAIRS, LAST_BASE)
            pool.wait_ge(stored[0], 16 * (PAIRS + 1))

        @block.scalar
        def _(act):
            def low(s, k):
                act.wait_ge(turned[s], k + 1)
                if began(k):
                    act.wait_ge(hid_done[s], k)
                nc.scalar.copy(hsT[s][:, 0:H], bank[0][:]).then_inc(hsT_low[s], 1)

            def relu(s, k):
                act.wait_ge(hid_done[s], k + 1)
                if began(k):
                    act.wait_ge(mlp_done[s], k)
                for i in range(2):
                    nc.scalar.activation(hid[s][:, i * H:(i + 1) * H], bank[2 + 2 * s + i][:], ACT.Relu,
                                         bias=c["ub1_col"][:, 0:1]).then_inc(hid_ready[s], 1)

            low(0, 0)
            for k in rounds(act, PAIRS):
                low(1, k)
                relu(0, k)
                low(0, k + 1)
                relu(1, k)
            relu(0, PAIRS)

        @block.vector
        def _(dve):
            def high(s, k):
                dve.wait_ge(turned[s], k + 1)
                if began(k):
                    dve.wait_ge(hid_done[s], k)
                nc.vector.tensor_copy(hsT[s][:, H:2 * H], bank[1][:]).then_inc(hsT_high[s], 1)

            def result(s, k):
                dve.wait_ge(mlp_done[s], k + 1)
                dve.wait_ge(x1_biased[s], k + 1)
                if began(k):
                    dve.wait_ge(stored[s], 16 * k)
                nc.vector.tensor_tensor(res[s][:], bank[6 + s][:].rearrange("p (r d) -> p r d", d=D), x1[s][:],
                                        ALU.add).then_inc(res_ready[s], 1)

            high(0, 0)
            for k in rounds(dve, PAIRS):
                high(1, k)
                result(0, k)
                high(0, k + 1)
                result(1, k)
            result(0, PAIRS)

        @block.tensor
        def _(pe):
            def turn(s, k, other):
                pe.wait_ge(hs_in[s], 16 * (k + 1))
                if began(other):
                    pe.wait_ge(hsT_low[1 - s], other)
                if began(other):
                    pe.wait_ge(hsT_high[1 - s], other)
                for r in range(R):
                    last = nc.tensor.transpose(bank[r // 4][:, (r % 4) * P:(r % 4 + 1) * P], hs[s][:, r].rearrange("p w d -> p (w d)"),
                                               c["ident"][:])
                last.then_inc(turned[s], 1)

            def first(s, k):
                pe.wait_ge(hsT_low[s], k + 1)
                pe.wait_ge(hsT_high[s], k + 1)
                if began(k):
                    pe.wait_ge(hid_ready[s], 2 * k)
                for i in range(2):
                    last = nc.tensor.matmul(bank[2 + 2 * s + i][:], c["uw1"][:], hsT[s][:, i * H:(i + 1) * H],
                                            start=True, stop=True)
                last.then_inc(hid_done[s], 1)

            def second(s, k):
                pe.wait_ge(hid_ready[s], 2 * (k + 1))
                if began(k):
                    pe.wait_ge(res_ready[s], k)
                for r in range(R):
                    last = nc.tensor.matmul(bank[6 + s][:, r * D:(r + 1) * D], hid[s][:, r * P:(r + 1) * P],
                                            c["uw2"][:], start=True, stop=True)
                last.then_inc(mlp_done[s], 1)

            turn(0, 0, 0)
            turn(1, 0, 1)
            first(0, 0)
            for k in rounds(pe, PAIRS - 1):
                turn(0, k + 1, k + 1)
                first(1, k)
                second(0, k)
                turn(1, k + 1, k + 2)
                first(0, k + 1)
                second(1, k)
            turn(0, PAIRS, PAIRS)
            first(1, PAIRS - 1)
            second(0, PAIRS - 1)
            first(0, PAIRS)
            second(1, PAIRS - 1)
            second(0, PAIRS)


_INS = ['x', 'src', 'dst', 'edge_weight', 'edge_weight_n2', 'L0_gnn_W', 'L0_gnn_b', 'L0_gnn_deg_coeff',
        'L0_gnn_coeff_param', 'L0_gnn_scale_param', 'L1_gnn_mW1', 'L1_gnn_mb1', 'L1_gnn_mW2', 'L1_gnn_mb2',
        'L1_gnn_uW1', 'L1_gnn_ub1', 'L1_gnn_uW2', 'L1_gnn_ub2']


def kernel(**inputs):
    import numpy as _np
    import concourse.bacc as _bacc
    from concourse import mybir as _mybir
    from concourse.bass_utils import run_bass_kernel_spmd as _run

    nc = _bacc.Bacc("TRN2", target_bir_lowering=False, num_devices=1)
    arrays, args = {}, []
    for name in _INS:
        a = _np.ascontiguousarray(inputs[name])
        arrays[f"in_{name}_dram"] = a
        args.append(nc.dram_tensor(f"in_{name}_dram", a.shape, _mybir.dt.from_np(a.dtype), kind="ExternalInput").ap())
    out = nc.dram_tensor("out_dram", (N, D), FP32, kind="ExternalOutput").ap()
    build(nc, *args, out)
    r = _run(nc, [arrays], core_ids=[0])
    return r.results[0]["out_dram"]
```

```python
import concourse.bass as bass
from concourse import mybir
from contextlib import ExitStack

FP32 = mybir.dt.float32
INT32 = mybir.dt.int32
BF16 = mybir.dt.bfloat16
ALU = mybir.AluOpType
ACT = mybir.ActivationFunctionType
AX = mybir.AxisListType

P = 128
N = 50000
E = 50000
D = 64
DH = 128
R = 8
BLOCK = P * R
BLOCKS = -(-N // BLOCK)
LAST_BASE = N - BLOCK
SLOTS = 6
ROUNDS = BLOCKS // SLOTS
G = 4
ESLOTS = 4
TILES = 392
GROUPS = TILES // G
WK = 3
WINDOW = P * WK
TRASH = N + P
ROWS = TRASH + G * P
SPARE = G + 1
CHUNKS = -(-TILES // P)
FULL = CHUNKS - 1
LAST_T = TILES - FULL * P
REST = E - FULL * P * P
REST_T, REST_E = REST // P, REST % P
EPS_LN = 1e-5
EPS_SIM = 1e-8

assert BLOCKS % SLOTS == 1 and SLOTS % 2 == 0 and GROUPS % 2 == 0 and TILES * P >= E and REST_E > 0


class Steps:

    def __init__(self, eng, sem, start=0):
        self.eng, self.sem, self.n, self.made = eng, sem, start, 0

    def mark(self, ins):
        self.n = self.n + 1
        self.made += 1
        ins.then_inc(self.sem, 1)

    def wait(self):
        self.eng.wait_ge(self.sem, self.n)

    def link(self, ins):
        self.mark(ins)
        self.wait()


def began(k):
    return not isinstance(k, int) or k > 0


def count(s, k, back=0, slots=0):
    return (slots or SLOTS) * k + s + 1 - back


def has(s, k, back, slots=0):
    return not isinstance(k, int) or count(s, k, back, slots) > 0


def rows_of(tab, base, r=R):
    return tab[bass.ds(base, P * r), :].rearrange("(p r) d -> p (r d)", r=r)


def build(nc, x, src, dst, edge_weight, edge_weight_n2, W, b, deg_coeff, coeff_param, scale_param,
          mW1, mb1, mW2, mb2, uW1, ub1, uW2, ub2, out):
    ctx = ExitStack()
    with ctx:
        def sb(name, shape, dt=FP32):
            return ctx.enter_context(nc.sbuf_tensor(name, shape, dt))

        def table(name, shape):
            return nc.dram_tensor(name, shape, FP32, kind="Internal").ap()

        tabs = {name: table(name, [ROWS, D]) for name in ("wh", "x1")}
        tabs["h1_agg"] = table("h1_agg", [2 * ROWS, D])
        tabs["ends"] = table("ends", [2, TILES, P])

        c = dict(
            held=ctx,
            ident=sb("ident", [P, P]),
            not_before=sb("not_before", [P, G * P]),
            near=sb("near", [1, 1], INT32),
            first_i=sb("first_i", [1, TILES], INT32),
            first_f=sb("first_f", [P, GROUPS, G]),
            in_window=sb("in_window", [P, WK]),
            zeros=sb("zeros", [P, 2 * SPARE * D]),
            eps_ln=sb("eps_ln", [P, 1]),
            trash=sb("trash", [P, G]),
            w_blk=sb("w_blk", [P, 2 * D]),
            b_rows=sb("b_rows", [1, R, D]),
            ones_row=sb("ones_row", [1, P]),
            mw1=sb("mw1", [P, DH]), mb1_col=sb("mb1_col", [P, 1]),
            mw2=sb("mw2", [P, D]), mb2_row=sb("mb2_row", [P, D]),
            uw1=sb("uw1", [P, DH]), ub1_col=sb("ub1_col", [P, 1]),
            uw2=sb("uw2", [P, D]), ub2_row=sb("ub2_row", [P, D]),
            mix=sb("mix", [P, 3]),
            edge_f=sb("edge_f", [P, 3, GROUPS, G]),
            edge_i=[sb(f"edge_i{layer}", [P, 2, GROUPS, G], INT32) for layer in range(2)],
            bank=[ctx.enter_context(nc.psum_tensor(f"bank{i}", [P, 512], FP32)) for i in range(8)],
        )
        prepare(nc, c, tabs, src, dst, edge_weight, edge_weight_n2, W, b, deg_coeff, coeff_param,
                scale_param, mW1, mb1, mW2, mb2, uW1, ub1, uW2, ub2)
        node_phase0(nc, c, tabs, x)
        edge_phase(nc, c, tabs, layer=0)
        node_phase1(nc, c, tabs)
        edge_phase(nc, c, tabs, layer=1)
        node_phase2(nc, c, tabs, out)


def prepare(nc, c, tabs, src, dst, edge_weight, edge_weight_n2, W, b, deg_coeff, coeff_param,
            scale_param, mW1, mb1, mW2, mb2, uW1, ub1, uW2, ub2):
    with ExitStack() as ctx:
        def sb(name, shape, dt=FP32):
            return ctx.enter_context(nc.sbuf_tensor(name, shape, dt))

        def sem(name):
            return c["held"].enter_context(nc.semaphore(name))

        rows_i = sb("rows_i", [P, 2, CHUNKS, P], INT32)
        rows_f = sb("rows_f", [P, 4, CHUNKS, P])
        trash_i = sb("trash_i", [P, G], INT32)
        in_window_i = sb("in_window_i", [P, WK], INT32)
        least, greatest, first, short = (sb(n, [P, CHUNKS]) for n in ("least", "greatest", "first", "short"))
        below_n = sb("below_n", [P, CHUNKS, P])
        ones_col = sb("ones_col", [P, 1])
        first_row = sb("first_row", [1, TILES])
        shorts = sb("shorts", [1, 1])
        TC = GROUPS * G
        adj = sb("adj", [P, TC])
        deg = sb("deg", [P, TC + 1])
        soft = [sb(f"soft{i}", [P, TC + 1]) for i in range(3)]
        differ = sb("differ", [P, TC])
        dc = sb("dc", [P, 2])
        cp = sb("cp", [P, 3])
        cps = [sb(f"cps{i}", [P, 3]) for i in range(4)]

        pads_made, rows_loaded, consts_loaded = sem("pads_made"), sem("rows_loaded"), sem("consts_loaded")
        pool_steps, pool_made, dve_steps = sem("pool_steps"), sem("pool_made"), sem("dve_steps")
        rows_ready, cols_done, soft_in, soft_exp, mix_in, mix_exp = (
            sem("rows_ready"), sem("cols_done"), sem("soft_in"), sem("soft_exp"), sem("mix_in"),
            sem("mix_exp"))
        stats_clear, first_ready, first_done, first_row_ready, first_spread = (
            sem("stats_clear"), sem("first_ready"), sem("first_done"), sem("first_row_ready"), sem("first_spread"))
        soft_log, cols_taken, ends_stored, blk_clear = (
            sem("soft_log"), sem("cols_taken"), sem("ends_stored"), sem("blk_clear"))

        with nc.Block() as block:
            @block.sync
            def _(sp):
                sp.wait_ge(pads_made, 4)
                n = 0
                for i, (rows, arr) in enumerate(((rows_i[:, 0], src), (rows_i[:, 1], dst),
                                                 (rows_f[:, 2], edge_weight),
                                                 (rows_f[:, 3], edge_weight_n2))):
                    whole = FULL * P * P
                    sp.dma_start(rows[:, 0:FULL, :],
                                 arr[0:whole].rearrange("(c q e) -> q c e", q=P, e=P)).then_inc(rows_loaded, 16)
                    sp.dma_start(rows[0:REST_T, FULL, :],
                                 arr[whole:whole + REST_T * P].rearrange("(q e) -> q e", e=P)).then_inc(rows_loaded, 16)
                    sp.dma_start(rows[REST_T:REST_T + 1, FULL, 0:REST_E],
                                 arr[whole + REST_T * P:E].rearrange("(q e) -> q e", q=1)).then_inc(rows_loaded, 16)
                sp.wait_ge(rows_ready, 1)
                for i in range(2):
                    sp.dma_start(tabs["ends"][i, 0:FULL * P, :].rearrange("(c q) e -> q c e", q=P),
                                 rows_f[:, i, 0:FULL, :]).then_inc(ends_stored, 16)
                    sp.dma_start(tabs["ends"][i, FULL * P:TILES, :],
                                 rows_f[0:LAST_T, i, FULL, :]).then_inc(ends_stored, 16)
                sp.wait_ge(ends_stored, 64)

            @block.scalar
            def _(act):
                act.wait_ge(blk_clear, 1)
                row = lambda v: v.rearrange("(a n) -> a n", a=1)
                col = lambda v: v.rearrange("(n a) -> n a", a=1)
                loads = [(c["w_blk"][0:D, 0:D], W), (c["w_blk"][D:2 * D, D:2 * D], W),
                         (c["mw1"][:], mW1), (c["mw2"][:], mW2), (c["uw1"][:], uW1), (c["uw2"][:], uW2),
                         (c["mb1_col"][:], col(mb1)), (c["ub1_col"][:], col(ub1)),
                         (c["b_rows"][:], row(b).unsqueeze(1).to_broadcast([1, R, D])),
                         (c["mb2_row"][:], row(mb2).to_broadcast([P, D])),
                         (c["ub2_row"][:], row(ub2).to_broadcast([P, D])),
                         (dc[:], row(deg_coeff).to_broadcast([P, 2])),
                         (cp[:], row(coeff_param).to_broadcast([P, 3])),
                         (deg[:, TC:TC + 1], row(scale_param).to_broadcast([P, 1]))]
                with nc.allow_non_contiguous_dma(reason="bias columns"):
                    for to, of in loads:
                        act.dma_start(to, of).then_inc(consts_loaded, 16)
                act.wait_ge(soft_in, 1)
                nc.scalar.activation(soft[1][:], soft[2][:], ACT.Exp, scale=-1.0).then_inc(soft_exp, 1)
                act.wait_ge(mix_in, 1)
                nc.scalar.activation(cps[1][:], cps[0][:], ACT.Exp).then_inc(mix_exp, 1)
                act.wait_ge(soft_exp, 1)
                nc.scalar.activation(soft[2][:], soft[1][:], ACT.Ln, bias=1.0).then_inc(soft_log, 1)

            @block.gpsimd
            def _(pool):
                steps = Steps(pool, pool_steps)
                for i in range(2):
                    nc.gpsimd.iota(rows_i[0:LAST_T, i, FULL, :], pattern=[[1, P]], base=N,
                                   channel_multiplier=0).then_inc(pads_made, 1)
                for i in range(2):
                    nc.gpsimd.memset(rows_f[0:LAST_T, 2 + i, FULL, :], 0.0).then_inc(pads_made, 1)
                nc.gpsimd.memset(c["w_blk"][:], 0.0).then_inc(blk_clear, 1)
                steps.mark(nc.gpsimd.memset(c["ident"][:], 0.0))
                steps.mark(nc.gpsimd.memset(c["not_before"][:], 1.0))
                for a, value in ((least, 0.0), (greatest, 0.0), (ones_col, 1.0)):
                    nc.gpsimd.memset(a[:], value).then_inc(stats_clear, 1)
                steps.mark(nc.gpsimd.iota(in_window_i[:], pattern=[[1, WK]], base=0, channel_multiplier=WK))
                steps.link(nc.gpsimd.iota(trash_i[:], pattern=[[P, G]], base=TRASH, channel_multiplier=1))
                nc.gpsimd.memset(c["ones_row"][:], 1.0).then_inc(pool_made, 1)
                nc.gpsimd.affine_select(out=c["ident"][:], in_=c["ident"][:], compare_op=ALU.not_equal,
                                        fill=1.0, base=0, pattern=[[-1, P]],
                                        channel_multiplier=1).then_inc(pool_made, 1)
                nc.gpsimd.affine_select(out=c["not_before"][:], in_=c["not_before"][:], compare_op=ALU.is_ge,
                                        fill=0.0, base=0, pattern=[[1, G * P]],
                                        channel_multiplier=-1).then_inc(pool_made, 1)
                nc.gpsimd.tensor_copy(c["trash"][:], trash_i[:]).then_inc(pool_made, 1)
                nc.gpsimd.tensor_copy(c["in_window"][:], in_window_i[:]).then_inc(pool_made, 1)
                nc.gpsimd.memset(c["zeros"][:], 0.0).then_inc(pool_made, 1)
                nc.gpsimd.memset(c["eps_ln"][:], EPS_LN).then_inc(pool_made, 1)

            @block.tensor
            def _(pe):
                pe.wait_ge(pool_made, 7)
                pe.wait_ge(rows_ready, 1)
                for i in range(4):
                    for ch in range(CHUNKS):
                        q = P if ch < FULL else LAST_T
                        last = nc.tensor.transpose(c["bank"][i][:, ch * P:ch * P + q],
                                                   rows_f[0:q, i, ch, :], c["ident"][0:q, 0:q])
                    last.then_inc(cols_done, 1)
                pe.wait_ge(first_ready, 1)
                pe.wait_ge(stats_clear, 3)
                for ch in range(CHUNKS):
                    q = P if ch < FULL else LAST_T
                    nc.tensor.transpose(c["bank"][4][0:1, ch * P:ch * P + q], first[0:q, ch:ch + 1],
                                        c["ident"][0:q, 0:q])
                nc.tensor.matmul(c["bank"][5][0:1, 0:CHUNKS], ones_col[:], short[:], start=True,
                                 stop=True).then_inc(first_done, 1)
                pe.wait_ge(first_row_ready, 1)
                nc.tensor.matmul(c["bank"][6][:, 0:TC], c["ones_row"][:], first_row[:], start=True,
                                 stop=True).then_inc(first_spread, 1)

            @block.vector
            def _(dve):
                steps = Steps(dve, dve_steps)
                dve.wait_ge(rows_loaded, 12 * 16)
                for i in range(2):
                    steps.mark(nc.vector.tensor_copy(rows_f[:, i, 0:FULL, :], rows_i[:, i, 0:FULL, :]))
                steps.mark(nc.vector.tensor_copy(rows_f[0:LAST_T, 0, FULL, :], rows_i[0:LAST_T, 0, FULL, :]))
                nc.vector.tensor_copy(rows_f[0:LAST_T, 1, FULL, :],
                                      rows_i[0:LAST_T, 1, FULL, :]).then_inc(rows_ready, 1)
                steps.wait()
                dve.wait_ge(rows_ready, 1)
                dve.wait_ge(stats_clear, 3)
                for q, ch in ((P, slice(0, FULL)), (LAST_T, slice(FULL, CHUNKS))):
                    steps.mark(nc.vector.tensor_reduce(least[0:q, ch], rows_f[0:q, 1, ch, :], AX.X, ALU.min))
                    steps.link(nc.vector.scalar_tensor_tensor(below_n[0:q, ch, :], rows_f[0:q, 1, ch, :], float(N),
                                                              rows_f[0:q, 1, ch, :], ALU.is_lt, ALU.mult))
                    steps.link(nc.vector.tensor_reduce(greatest[0:q, ch], below_n[0:q, ch, :], AX.X, ALU.max))
                steps.link(nc.vector.tensor_scalar(first[:], least[:], float(ROWS - WINDOW), None, ALU.min))
                steps.link(nc.vector.tensor_tensor(greatest[:], greatest[:], first[:], ALU.subtract))
                nc.vector.tensor_scalar(short[:], greatest[:], WINDOW - 0.5, None, ALU.is_gt).then_inc(first_ready, 1)
                dve.wait_ge(first_done, 1)
                nc.vector.tensor_copy(first_row[:], c["bank"][4][0:1, 0:TC]).then_inc(first_row_ready, 1)
                steps.mark(nc.vector.tensor_copy(c["first_i"][:], c["bank"][4][0:1, 0:TC]))
                steps.link(nc.vector.tensor_reduce(shorts[:], c["bank"][5][0:1, 0:CHUNKS], AX.X, ALU.add))
                steps.mark(nc.vector.tensor_scalar(c["near"][:], shorts[:], 0.5, None, ALU.is_lt))
                dve.wait_ge(first_spread, 1)
                steps.mark(nc.vector.tensor_copy(c["first_f"][:].rearrange("p g j -> p (g j)"), c["bank"][6][:, 0:TC]))
                dve.wait_ge(cols_done, 4)
                ef = c["edge_f"]
                flat = lambda a: a.rearrange("p g j -> p (g j)")
                for i in range(2):
                    steps.mark(nc.vector.tensor_copy(flat(ef[:, i, 0:GROUPS, :]), c["bank"][i][:, 0:TC]))
                    steps.mark(nc.vector.tensor_copy(flat(c["edge_i"][0][:, i, 0:GROUPS, :]), c["bank"][i][:, 0:TC]))
                    steps.mark(nc.vector.tensor_scalar(flat(c["edge_i"][1][:, i, 0:GROUPS, :]), c["bank"][i][:, 0:TC],
                                                       2.0, None, ALU.mult))
                steps.mark(nc.vector.tensor_copy(adj[:], c["bank"][2][:, 0:TC]))
                dve.wait_ge(consts_loaded, 14 * 16)
                steps.mark(nc.vector.tensor_scalar(soft[0][:, 0:TC], c["bank"][3][:, 0:TC], dc[:, 0:1], dc[:, 1:2],
                                                   ALU.mult, ALU.add))
                steps.link(nc.vector.tensor_copy(soft[0][:, TC:TC + 1], deg[:, TC:TC + 1]))
                nc.vector.scalar_tensor_tensor(soft[2][:], soft[0][:], -1.0, soft[0][:], ALU.mult, ALU.max).then_inc(soft_in, 1)
                steps.link(nc.vector.tensor_reduce(cps[3][:, 0:1], cp[:], AX.X, ALU.max))
                nc.vector.tensor_scalar(cps[0][:], cp[:], cps[3][:, 0:1], None, ALU.subtract).then_inc(mix_in, 1)
                steps.link(nc.vector.tensor_tensor(differ[:], flat(ef[:, 0, 0:GROUPS, :]),
                                                   flat(ef[:, 1, 0:GROUPS, :]), ALU.not_equal))
                steps.link(nc.vector.tensor_tensor(adj[:], adj[:], differ[:], ALU.mult))
                dve.wait_ge(mix_exp, 1)
                steps.link(nc.vector.tensor_reduce(cps[3][:, 1:2], cps[1][:], AX.X, ALU.add))
                steps.link(nc.vector.reciprocal(cps[3][:, 2:3], cps[3][:, 1:2]))
                steps.link(nc.vector.tensor_scalar(cps[2][:], cps[1][:], cps[3][:, 2:3], None, ALU.mult))
                dve.wait_ge(soft_log, 1)
                steps.link(nc.vector.scalar_tensor_tensor(soft[1][:], soft[0][:], 0.0, soft[2][:],
                                                          ALU.max, ALU.add))
                steps.mark(nc.vector.tensor_tensor(flat(ef[:, 2, 0:GROUPS, :]), adj[:], soft[1][:, 0:TC], ALU.mult))
                steps.link(nc.vector.tensor_scalar(c["mix"][:], cps[2][:], soft[1][:, TC:TC + 1], None, ALU.mult))


def rounds_of_blocks(eng, parts, slots=0, blocks=0):
    slots, blocks = slots or SLOTS, blocks or BLOCKS
    full = blocks // slots
    lag = -min(offset for offset, _ in parts)
    first = 1 + max(1, -(-lag // slots))

    def steps(k):
        for j in range(slots):
            for offset, part in parts:
                s, r = (j + offset) % slots, k + (j + offset) // slots
                if not isinstance(k, int) or 0 <= r * slots + s < blocks:
                    part(s, r)

    for k in range(first):
        steps(k)
    with eng.Fori(first, full) as k:
        steps(k)
    for k in range(full, full + first + 1):
        steps(k)


def base_of(s, k):
    if isinstance(k, int) and k * SLOTS + s == BLOCKS - 1:
        return LAST_BASE
    return (k * SLOTS + s) * BLOCK


def rows(a):
    return a.rearrange("p (r d) -> p r d", d=D)


def by_row(a):
    return a.unsqueeze(2).to_broadcast([P, R, D])


class Slots:

    def __init__(self, nc, c, ctx, tag):
        self.nc, self.ctx, self.tag, self.held, self.made = nc, ctx, tag, c["held"], []

    def bufs(self, name, shape, n=SLOTS, dt=FP32):
        return [self.ctx.enter_context(self.nc.sbuf_tensor(f"{self.tag}_{name}{s}", shape, dt)) for s in range(n)]

    def sem(self, name):
        self.made.append(self.held.enter_context(self.nc.semaphore(f"{self.tag}_{name}")))
        return self.made[-1]

    def sems(self, name, n=SLOTS):
        return [self.sem(f"{name}{s}") for s in range(n)]


class LayerNorm:

    def __init__(self, nc, c, slots, h):
        self.nc, self.c, self.h = nc, c, h
        self.x, self.xc, self.sq = (slots.bufs(n, [P, R * D]) for n in ("x", "xc", "sq"))
        self.total, self.mean, self.ssq, self.std, self.rstd = (
            slots.bufs(n, [P, R]) for n in ("total", "mean", "ssq", "std", "rstd"))
        self.x_in = slots.sems("x_in")
        (self.total_ready, self.mean_ready, self.xc_ready, self.sq_ready, self.ssq_ready,
         self.std_ready, self.rstd_ready, self.h_ready) = (
            slots.sem(n) for n in ("total_ready", "mean_ready", "xc_ready", "sq_ready", "ssq_ready",
                                    "std_ready", "rstd_ready", "h_ready"))

    def dve_mean(self, dve, s, k):
        dve.wait_ge(self.x_in[s], 16 * (k + 1))
        self.nc.vector.tensor_reduce(self.total[s][:], rows(self.x[s][:]), AX.X,
                                     ALU.add).then_inc(self.total_ready, 1)
        dve.wait_ge(self.total_ready, count(s, k))
        self.nc.vector.tensor_scalar(self.mean[s][:], self.total[s][:], 1.0 / D, None,
                                     ALU.mult).then_inc(self.mean_ready, 1)

    def pool_centre(self, pool, s, k):
        pool.wait_ge(self.mean_ready, count(s, k))
        if began(k):
            pool.wait_ge(self.h_ready, count(s, k, SLOTS))
        self.nc.gpsimd.tensor_tensor(rows(self.xc[s][:]), rows(self.x[s][:]), by_row(self.mean[s][:]),
                                     ALU.subtract).then_inc(self.xc_ready, 1)

    def act_square(self, act, s, k):
        act.wait_ge(self.xc_ready, count(s, k))
        if began(k):
            act.wait_ge(self.ssq_ready, count(s, k, SLOTS))
        self.nc.scalar.activation(self.sq[s][:], self.xc[s][:], ACT.Square).then_inc(self.sq_ready, 1)

    def dve_squares(self, dve, s, k):
        dve.wait_ge(self.sq_ready, count(s, k))
        self.nc.vector.tensor_reduce(self.ssq[s][:], rows(self.sq[s][:]), AX.X,
                                     ALU.add).then_inc(self.ssq_ready, 1)

    def act_std(self, act, s, k):
        act.wait_ge(self.ssq_ready, count(s, k))
        self.nc.scalar.activation(self.std[s][:], self.ssq[s][:], ACT.Sqrt, bias=self.c["eps_ln"][:, 0:1],
                                  scale=1.0 / D).then_inc(self.std_ready, 1)

    def dve_h(self, dve, s, k):
        dve.wait_ge(self.std_ready, count(s, k))
        self.nc.vector.reciprocal(self.rstd[s][:], self.std[s][:]).then_inc(self.rstd_ready, 1)
        dve.wait_ge(self.rstd_ready, count(s, k))
        self.nc.vector.scalar_tensor_tensor(self.h[s], rows(self.xc[s][:]), 0.0, by_row(self.rstd[s][:]),
                                            ALU.max, ALU.mult).then_inc(self.h_ready, 1)


def node_phase0(nc, c, tabs, x):
    with ExitStack() as ctx:
        slots = Slots(nc, c, ctx, "n0")
        h, hT, wh, x1 = (slots.bufs(n, [P, R * D]) for n in ("h", "hT", "wh", "x1"))
        ln = LayerNorm(nc, c, slots, [rows(a[:]) for a in h])
        stored = slots.sems("stored")
        turned, hT_ready, wh_done, wh_ready, x1_ready = (
            slots.sem(n) for n in ("turned", "hT_ready", "wh_done", "wh_ready", "x1_ready"))
        pads_stored = c["held"].enter_context(nc.semaphore("n0_pads_stored"))
        turn_bank, wh_bank = c["bank"][0:2], c["bank"][2:4]
        block = ctx.enter_context(nc.Block())

        @block.sync
        def _(sp):
            for name in ("wh", "x1"):
                sp.dma_start(rows_of(tabs[name], N, SPARE), c["zeros"][:, 0:SPARE * D]).then_inc(pads_stored, 16)
            sp.dma_start(rows_of(tabs["h1_agg"], 2 * N, 2 * SPARE), c["zeros"][:]).then_inc(pads_stored, 16)

            def store(s, k):
                sp.wait_ge(x1_ready, count(s, k))
                sp.wait_ge(wh_ready, count(s, k))
                base = base_of(s, k)
                if base is LAST_BASE:
                    sp.wait_ge(stored[SLOTS - 1], 32 * k)
                sp.dma_start(rows_of(tabs["wh"], base), wh[s][:]).then_inc(stored[s], 16)
                sp.dma_start(rows_of(tabs["x1"], base), x1[s][:]).then_inc(stored[s], 16)

            def load(s, k):
                if began(k):
                    sp.wait_ge(x1_ready, count(s, k, SLOTS))
                sp.dma_start(ln.x[s][:], rows_of(x, base_of(s, k))).then_inc(ln.x_in[s], 16)

            rounds_of_blocks(sp, [(-SLOTS, store), (0, load)])
            sp.wait_ge(pads_stored, 48)
            for s in range(SLOTS):
                sp.wait_ge(stored[s], 32 * (ROUNDS + (s == 0)))

        @block.vector
        def _(dve):
            def mean(s, k):
                ln.dve_mean(dve, s, k)

            def squares(s, k):
                ln.dve_squares(dve, s, k)

            def normed(s, k):
                if began(k):
                    dve.wait_ge(turned, count(s, k, SLOTS))
                ln.dve_h(dve, s, k)

            def begin_x1(s, k):
                dve.wait_ge(wh_ready, count(s, k))
                if began(k):
                    dve.wait_ge(stored[s], 32 * k)
                nc.vector.scalar_tensor_tensor(x1[s][:], wh[s][:], c["mix"][:, 2:3], ln.x[s][:],
                                               ALU.mult, ALU.add).then_inc(x1_ready, 1)

            rounds_of_blocks(dve, [(0, mean), (-1, squares), (-4, begin_x1), (-1, normed)])

        @block.gpsimd
        def _(pool):
            rounds_of_blocks(pool, [(0, lambda s, k: ln.pool_centre(pool, s, k))])

        @block.scalar
        def _(act):
            def copy_hT(s, k):
                act.wait_ge(turned, count(s, k))
                if began(k):
                    act.wait_ge(wh_done, count(s, k, SLOTS))
                nc.scalar.copy(hT[s][:], turn_bank[s % 2][:]).then_inc(hT_ready, 1)

            def copy_wh(s, k):
                act.wait_ge(wh_done, count(s, k))
                if began(k):
                    act.wait_ge(stored[s], 32 * k)
                nc.scalar.copy(wh[s][:], wh_bank[s % 2][:]).then_inc(wh_ready, 1)

            rounds_of_blocks(act, [(-1, lambda s, k: ln.act_std(act, s, k)), (0, lambda s, k: ln.act_square(act, s, k)),
                                   (-3, copy_wh), (-2, copy_hT)])

        @block.tensor
        def _(pe):
            def turn(s, k):
                pe.wait_ge(ln.h_ready, count(s, k))
                if has(s, k, 2):
                    pe.wait_ge(hT_ready, count(s, k, 2))
                for q in range(R // 2):
                    last = nc.tensor.transpose(turn_bank[s % 2][:, q * P:(q + 1) * P],
                                               h[s][:, q * 2 * D:(q + 1) * 2 * D], c["ident"][:])
                last.then_inc(turned, 1)

            def multiply(s, k):
                pe.wait_ge(hT_ready, count(s, k))
                if has(s, k, 2):
                    pe.wait_ge(wh_ready, count(s, k, 2))
                nc.tensor.matmul(wh_bank[s % 2][:], c["ones_row"][:], c["b_rows"][:].rearrange("p r d -> p (r d)"), start=True, stop=False)
                for q in range(R // 2):
                    last = nc.tensor.matmul(wh_bank[s % 2][:, q * P:(q + 1) * P], hT[s][:, q * P:(q + 1) * P],
                                            c["w_blk"][:], start=False, stop=q == R // 2 - 1)
                last.then_inc(wh_done, 1)

            rounds_of_blocks(pe, [(-1, turn), (-2, multiply)])


def node_phase1(nc, c, tabs):
    with ExitStack() as ctx:
        slots = Slots(nc, c, ctx, "n1")
        h_agg = slots.bufs("h_agg", [P, R, 2, D])
        ln = LayerNorm(nc, c, slots, [a[:, :, 0, :] for a in h_agg])
        stored = slots.sems("stored")
        halves_zero = c["held"].enter_context(nc.semaphore("n1_halves_zero"))
        block = ctx.enter_context(nc.Block())

        @block.sync
        def _(sp):
            sp.wait_ge(halves_zero, SLOTS)

            def store(s, k):
                sp.wait_ge(ln.h_ready, count(s, k))
                base = base_of(s, k)
                if base is LAST_BASE:
                    sp.wait_ge(stored[SLOTS - 1], 16 * k)
                sp.dma_start(rows_of(tabs["h1_agg"], 2 * base, 2 * R),
                             h_agg[s][:].rearrange("p r w d -> p (r w d)")).then_inc(stored[s], 16)

            def load(s, k):
                if began(k):
                    sp.wait_ge(ln.xc_ready, count(s, k, SLOTS))
                sp.dma_start(ln.x[s][:], rows_of(tabs["x1"], base_of(s, k))).then_inc(ln.x_in[s], 16)

            rounds_of_blocks(sp, [(1 - SLOTS, store), (0, load)])
            for s in range(SLOTS):
                sp.wait_ge(stored[s], 16 * (ROUNDS + (s == 0)))

        @block.vector
        def _(dve):
            def normed(s, k):
                if began(k):
                    dve.wait_ge(stored[s], 16 * k)
                ln.dve_h(dve, s, k)

            rounds_of_blocks(dve, [(0, lambda s, k: ln.dve_mean(dve, s, k)),
                                   (-2, lambda s, k: ln.dve_squares(dve, s, k)), (-3, normed)])

        @block.gpsimd
        def _(pool):
            for s in range(SLOTS):
                nc.gpsimd.memset(h_agg[s][:, :, 1, :], 0.0).then_inc(halves_zero, 1)
            rounds_of_blocks(pool, [(0, lambda s, k: ln.pool_centre(pool, s, k))])

        @block.scalar
        def _(act):
            rounds_of_blocks(act, [(-2, lambda s, k: ln.act_std(act, s, k)), (0, lambda s, k: ln.act_square(act, s, k))])


def edge_phase(nc, c, tabs, layer):
    with ExitStack() as ctx:
        slots = Slots(nc, dict(held=ctx), ctx, f"e{layer}")
        t = EdgeBuffers(slots, layer)
        with nc.Block() as block:
            edge_programs(nc, block, c, tabs, t, layer)
        with nc.Block() as block:
            @block.sync
            def _(sp):
                for sem in slots.made:
                    sp.sem_clear(sem)


def edge_programs(nc, block, c, tabs, t, layer):
    def both_ways(eng, program):
        near = eng.value_load(c["near"][0:1, 0:1], min_val=0, max_val=1)
        with eng.If(near > 0):
            program(True)
        with eng.Else():
            program(False)

    @block.sync
    def _(sp):
        both_ways(sp, lambda near: edge_loads(nc, sp, c, tabs, t, layer, near))

    @block.gpsimd
    def _(pool):
        both_ways(pool, lambda near: edge_pool(nc, pool, c, tabs, t, layer, near))

    @block.vector
    def _(dve):
        both_ways(dve, lambda near: edge_vector(nc, dve, c, t, layer, near))

    @block.scalar
    def _(act):
        both_ways(act, lambda near: edge_scalar(nc, act, c, t, layer, near))

    @block.tensor
    def _(pe):
        both_ways(pe, lambda near: edge_tensor(nc, pe, c, t, layer, near))


class EdgeBuffers:
    def __init__(self, slots, layer):
        def bufs(name, shape, dt=FP32):
            return slots.bufs(name, shape, ESLOTS, dt)

        self.src_at = layer
        self.dst_at = 1 - layer
        self.owners = bufs("owners", [P, G * P])
        self.targets = bufs("targets", [P, G * P]) if layer == 0 else self.owners
        self.window = bufs("window", [P, G, WK, D])
        self.window_row = bufs("window_row", [P, G, WK])
        self.onehot = bufs("onehot", [P, G, WK, P])
        self.ids = bufs("ids", [P, 2, G], INT32)
        self.ef = bufs("ef", [P, 3, G])
        self.ends = bufs("ends", [P, G, 2, D])
        self.same = bufs("same", [P, G * (G + 1) // 2, P], BF16)
        self.later = bufs("later", [P, G])
        self.trashed = bufs("trashed", [P, 3, G])
        self.to = bufs("to", [P, G], INT32)
        self.msgs, self.sums = bufs("msgs", [P, G, D]), bufs("sums", [P, G, D])
        self.parts, self.left = bufs("parts", [P, 3, G, D], BF16), bufs("left", [P, G, D])
        if layer == 0:
            self.prod, self.sq = bufs("prod", [P, G, D]), bufs("sq", [P, G, 2, D])
            self.dot, self.norm2, self.norm = bufs("dot", [P, G]), bufs("norm2", [P, G, 2]), bufs("norm", [P, G, 2])
            self.small = bufs("small", [P, 7, G])
        else:
            self.endsT, self.hid = bufs("endsT", [P, G * P]), bufs("hid", [P, G * P])
        self.numbers_in, self.window_in, self.gathered, self.added = (
            slots.sems(n, ESLOTS) for n in ("numbers_in", "window_in", "gathered", "added"))
        (self.onehot_ready, self.found, self.found_ready, self.same_ready, self.ids_ready, self.to_ready,
         self.msgs_ready, self.summed, self.sums_ready, self.steps, self.waited, self.row_ready,
         self.ef_ready, self.apart_ready, self.away_ready, self.row_at,
         self.high_ready, self.left_ready, self.mid_ready, self.low_ready) = (
            slots.sem(n) for n in ("onehot_ready", "found", "found_ready", "same_ready", "ids_ready", "to_ready",
                                   "msgs_ready", "summed", "sums_ready", "steps", "waited", "row_ready",
                                   "ef_ready", "apart_ready", "away_ready", "row_at",
                                   "high_ready", "left_ready", "mid_ready", "low_ready"))
        if layer == 0:
            self.norm2_ready, self.norm_ready = (
                slots.sem(n) for n in ("norm2_ready", "norm_ready"))
        else:
            self.turned, self.endsT_ready, self.hid_done, self.hid_ready, self.mlp_done = (
                slots.sem(n) for n in ("turned", "endsT_ready", "hid_done", "hid_ready", "mlp_done"))
        self.ends_used = self.msgs_ready if layer == 0 else self.turned

    def numbers(self, eng, s, k, near):
        eng.wait_ge(self.numbers_in[s], 16 * (2 if near and self.targets is not self.owners else 1) * (k + 1))

    def all_gathered(self, eng, s, k, near):
        eng.wait_ge(self.gathered[s], 16 * G * (1 if near else 2) * (k + 1))


def same_block(j, i):
    return j * G - j * (j - 1) // 2 + (i - j)


def edge_loads(nc, sp, c, tabs, t, layer, near):
    def numbers(s, k, end):
        return tabs["ends"][end, bass.ds((ESLOTS * k + s) * G, G), :].rearrange("t e -> (t e)").partition_broadcast(P)

    def load(s, k):
        if has(s, k, ESLOTS, ESLOTS):
            sp.wait_ge(t.same_ready, G * count(s, k, ESLOTS, ESLOTS))
            if near:
                sp.wait_ge(t.onehot_ready, count(s, k, ESLOTS, ESLOTS))
        sp.dma_start(t.owners[s][:], numbers(s, k, layer)).then_inc(t.numbers_in[s], 16)
        if not near:
            return
        if layer == 0:
            sp.dma_start(t.targets[s][:], numbers(s, k, 1)).then_inc(t.numbers_in[s], 16)
        if has(s, k, ESLOTS, ESLOTS):
            sp.wait_ge(t.found, count(s, k, ESLOTS, ESLOTS))
        for j in range(G):
            first = sp.value_load(c["first_i"][0:1, bass.ds((ESLOTS * k + s) * G + j, 1)], min_val=0,
                                  max_val=ROWS - WINDOW)
            if layer == 0:
                rows = tabs["wh"][bass.ds(first, WINDOW), :].rearrange("(p w) d -> p w d", w=WK)
            else:
                rows = tabs["h1_agg"].rearrange("(n w) d -> n w d", w=2)[bass.ds(first, WINDOW), 0, :].rearrange(
                    "(p w) d -> p w d", w=WK)
            sp.dma_start(t.window[s][:, j], rows).then_inc(t.window_in[s], 16)

    rounds_of_blocks(sp, [(0, load)], ESLOTS, GROUPS)


def edge_pool(nc, pool, c, tabs, t, layer, near):
    gathered_tab = tabs["wh"] if layer == 0 else tabs["h1_agg"]
    added_tab = tabs["x1"] if layer == 0 else tabs["h1_agg"]

    def gather(s, k):
        pool.wait_ge(t.ids_ready, count(s, k, 0, ESLOTS))
        if has(s, k, ESLOTS, ESLOTS):
            pool.wait_ge(t.ends_used, count(s, k, ESLOTS, ESLOTS))
        pool.sem_inc(t.waited, 1)
        for j in range(G):
            for end, at in ((0, t.src_at), (1, t.dst_at))[:1 if near else 2]:
                pool.indirect_dma_start(
                    out=t.ends[s][:, j, at, :], out_offset=None, in_=gathered_tab,
                    in_offset=bass.IndirectOffsetOnAxis(ap=t.ids[s][:, end, j:j + 1], axis=0),
                ).then_inc(t.gathered[s], 16)

    def scatter(s, k):
        pool.wait_ge(t.to_ready, count(s, k, 0, ESLOTS))
        pool.wait_ge(t.sums_ready, count(s, k, 0, ESLOTS))
        if s:
            pool.wait_ge(t.added[s - 1], 16 * G * (k + 1))
        elif began(k):
            pool.wait_ge(t.added[ESLOTS - 1], 16 * G * k)
        pool.sem_inc(t.waited, 1)
        for j in range(G):
            pool.indirect_dma_start(
                out=added_tab, out_offset=bass.IndirectOffsetOnAxis(ap=t.to[s][:, j:j + 1], axis=0),
                in_=t.sums[s][:, j, :], in_offset=None, compute_op=ALU.add).then_inc(t.added[s], 16)

    rounds_of_blocks(pool, [(0, gather), (-3, scatter)], ESLOTS, GROUPS)
    for s in range(ESLOTS):
        pool.wait_ge(t.added[s], 16 * G * -(-(GROUPS - s) // ESLOTS))


def edge_vector(nc, dve, c, t, layer, near):
    dot_steps, weigh_steps = G, 8

    def of_group(a, s, k):
        return a[:, :, bass.ds(ESLOTS * k + s, 1), :].rearrange("p w a j -> p w (a j)")

    def ahead(s, k):
        if has(s, k, ESLOTS, ESLOTS):
            t.all_gathered(dve, s, k - 1, near)
        nc.vector.tensor_copy(t.ids[s][:], of_group(c["edge_i"][layer], s, k)).then_inc(t.ids_ready, 1)
        if not near:
            return
        group = c["first_f"][:, bass.ds(ESLOTS * k + s, 1), :].rearrange("p a j -> p (a j)")
        nc.vector.tensor_tensor(
            t.window_row[s][:], group.unsqueeze(2).to_broadcast([P, G, WK]),
            c["in_window"][:, :].unsqueeze(1).to_broadcast([P, G, WK]), ALU.add).then_inc(t.row_ready, 1)
        dve.wait_ge(t.row_ready, count(s, k, 0, ESLOTS))
        t.numbers(dve, s, k, near)
        if has(s, k, ESLOTS, ESLOTS):
            dve.wait_ge(t.found, count(s, k, ESLOTS, ESLOTS))
        nc.vector.tensor_tensor(
            t.onehot[s][:], t.targets[s][:].rearrange("p (j e) -> p j e", e=P).unsqueeze(2).to_broadcast([P, G, WK, P]),
            t.window_row[s][:].unsqueeze(3).to_broadcast([P, G, WK, P]), ALU.is_equal).then_inc(t.onehot_ready, 1)

    def match(s, k):
        if has(s, k, ESLOTS, ESLOTS):
            dve.wait_ge(t.to_ready, count(s, k, ESLOTS, ESLOTS))
        nc.vector.tensor_copy(t.ef[s][:], of_group(c["edge_f"], s, k)).then_inc(t.ef_ready, 1)
        owner = t.ef[s][:, layer, :]
        dve.wait_ge(t.ef_ready, count(s, k, 0, ESLOTS))
        t.numbers(dve, s, k, near)
        if has(s, k, ESLOTS, ESLOTS):
            dve.wait_ge(t.summed, count(s, k, ESLOTS, ESLOTS))
        for j in range(G):
            n = (G - j) * P
            nc.vector.scalar_tensor_tensor(
                t.same[s][:, same_block(j, j):same_block(j, G - 1) + 1, :].rearrange("p b i -> p (b i)"),
                t.owners[s][:, j * P:], owner[:, j:j + 1], c["not_before"][:, 0:n],
                ALU.is_equal, ALU.mult, accum_out=t.later[s][:, j:j + 1]).then_inc(t.same_ready, 1)
        nc.vector.tensor_tensor(t.trashed[s][:, 0, :], c["trash"][:], owner, ALU.subtract).then_inc(t.apart_ready, 1)

    def own_steps(s, k, before):
        return Steps(dve, t.steps, (dot_steps + weigh_steps) * (count(s, k, 0, ESLOTS) - 1) + before)

    def compare(s, k):
        steps = own_steps(s, k, 0)
        t.all_gathered(dve, s, k, near)
        if near:
            dve.wait_ge(t.found_ready, count(s, k, 0, ESLOTS))
        for j in range(G):
            steps.mark(nc.vector.scalar_tensor_tensor(
                t.prod[s][:, j], t.ends[s][:, j, 0, :], 1.0, t.ends[s][:, j, 1, :], ALU.mult, ALU.mult,
                accum_out=t.dot[s][:, j:j + 1]))
        assert steps.made == dot_steps

    def weigh(s, k):
        steps = own_steps(s, k, dot_steps)
        a = t.small[s]
        dve.wait_ge(t.norm_ready, count(s, k, 0, ESLOTS))
        steps.link(nc.vector.tensor_tensor(a[:, 0, :], t.norm[s][:, :, 0], t.norm[s][:, :, 1], ALU.mult))
        steps.link(nc.vector.tensor_scalar(a[:, 1, :], a[:, 0, :], EPS_SIM, None, ALU.max))
        steps.link(nc.vector.reciprocal(a[:, 2, :], a[:, 1, :]))
        steps.link(nc.vector.tensor_tensor(a[:, 3, :], t.dot[s][:], a[:, 2, :], ALU.mult))
        steps.mark(nc.vector.tensor_scalar(a[:, 4, :], a[:, 3, :], 0.0, c["mix"][:, 0:1], ALU.max, ALU.mult))
        steps.link(nc.vector.tensor_scalar(a[:, 5, :], a[:, 3, :], 0.0, c["mix"][:, 1:2], ALU.min, ALU.mult))
        steps.link(nc.vector.tensor_tensor(a[:, 6, :], a[:, 4, :], a[:, 5, :], ALU.add))
        steps.link(nc.vector.tensor_tensor(a[:, 0, :], a[:, 6, :], t.ef[s][:, 2, :], ALU.mult))
        nc.vector.tensor_tensor(t.msgs[s][:], t.ends[s][:, :, 1, :], a[:, 0, :].unsqueeze(2).to_broadcast([P, G, D]),
                                ALU.mult).then_inc(t.msgs_ready, 1)
        assert steps.made == weigh_steps

    def bias(s, k):
        dve.wait_ge(t.mlp_done, count(s, k, 0, ESLOTS))
        nc.vector.tensor_tensor(t.msgs[s][:], c["bank"][4 + s % 2][:, 0:G * D].rearrange("p (j d) -> p j d", d=D),
                                c["mb2_row"][:, :].unsqueeze(1).to_broadcast([P, G, D]),
                                ALU.add).then_inc(t.msgs_ready, 1)

    def leave(s, k):
        dve.wait_ge(t.high_ready, count(s, k, 0, ESLOTS))
        nc.vector.tensor_tensor(t.left[s][:], t.msgs[s][:], t.parts[s][:, 0], ALU.subtract).then_inc(t.left_ready, 1)

    def low(s, k):
        dve.wait_ge(t.mid_ready, count(s, k, 0, ESLOTS))
        nc.vector.tensor_tensor(t.parts[s][:, 2], t.left[s][:], t.parts[s][:, 1], ALU.subtract).then_inc(t.low_ready, 1)

    def address(s, k):
        owner = t.ef[s][:, layer, :]
        dve.wait_ge(t.same_ready, G * count(s, k, 0, ESLOTS))
        dve.wait_ge(t.apart_ready, count(s, k, 0, ESLOTS))
        nc.vector.scalar_tensor_tensor(t.trashed[s][:, 1, :], t.later[s][:], 1.5, t.trashed[s][:, 0, :],
                                       ALU.is_gt, ALU.mult).then_inc(t.away_ready, 1)
        dve.wait_ge(t.away_ready, count(s, k, 0, ESLOTS))
        if has(s, k, ESLOTS, ESLOTS):
            dve.wait_ge(t.added[s], 16 * G * k)
        if layer == 0:
            nc.vector.tensor_tensor(t.to[s][:], t.trashed[s][:, 1, :], owner, ALU.add).then_inc(t.to_ready, 1)
        else:
            nc.vector.tensor_tensor(t.trashed[s][:, 2, :], t.trashed[s][:, 1, :], owner, ALU.add).then_inc(t.row_at, 1)
            dve.wait_ge(t.row_at, count(s, k, 0, ESLOTS))
            nc.vector.tensor_scalar(t.to[s][:], t.trashed[s][:, 2, :], 2.0, 1.0, ALU.mult,
                                    ALU.add).then_inc(t.to_ready, 1)

    if layer == 0:
        parts = [(-3, leave), (0, ahead), (-3, low), (-1, match), (-2, compare), (-2, address), (-2, weigh)]
    else:
        parts = [(-3, low), (0, ahead), (-1, match), (-2, address), (-2, bias), (-2, leave)]
    rounds_of_blocks(dve, parts, ESLOTS, GROUPS)


def edge_scalar(nc, act, c, t, layer, near):
    bank = c["bank"]

    def found(s, k):
        act.wait_ge(t.found, count(s, k, 0, ESLOTS))
        if has(s, k, ESLOTS, ESLOTS):
            act.wait_ge(t.ends_used, count(s, k, ESLOTS, ESLOTS))
        nc.scalar.copy(t.ends[s][:, :, t.dst_at, :],
                       bank[s % 2][:, 0:G * D].rearrange("p (j d) -> p j d", d=D)).then_inc(t.found_ready, 1)

    def norms(s, k):
        t.all_gathered(act, s, k, near)
        if near:
            act.wait_ge(t.found_ready, count(s, k, 0, ESLOTS))
        if has(s, k, ESLOTS, ESLOTS):
            act.wait_ge(t.msgs_ready, count(s, k, ESLOTS, ESLOTS))
        for j in range(G):
            for end in range(2):
                nc.scalar.activation(t.sq[s][:, j, end, :], t.ends[s][:, j, end, :], ACT.Square,
                                     accum_out=t.norm2[s][:, j, end:end + 1]).then_inc(t.norm2_ready, 1)
        act.wait_ge(t.norm2_ready, 2 * G * count(s, k, 0, ESLOTS))
        nc.scalar.activation(t.norm[s][:], t.norm2[s][:], ACT.Sqrt).then_inc(t.norm_ready, 1)

    def copy_ends(s, k):
        act.wait_ge(t.turned, count(s, k, 0, ESLOTS))
        nc.scalar.copy(t.endsT[s][:], bank[s % 2][:]).then_inc(t.endsT_ready, 1)

    def relu(s, k):
        act.wait_ge(t.hid_done, count(s, k, 0, ESLOTS))
        nc.scalar.activation(t.hid[s][:], bank[2 + s % 2][:], ACT.Relu,
                             bias=c["mb1_col"][:, 0:1]).then_inc(t.hid_ready, 1)

    def high(s, k):
        act.wait_ge(t.msgs_ready, count(s, k, 0, ESLOTS))
        if has(s, k, ESLOTS, ESLOTS):
            act.wait_ge(t.summed, count(s, k, ESLOTS, ESLOTS))
        nc.scalar.copy(t.parts[s][:, 0], t.msgs[s][:]).then_inc(t.high_ready, 1)

    def mid(s, k):
        act.wait_ge(t.left_ready, count(s, k, 0, ESLOTS))
        nc.scalar.copy(t.parts[s][:, 1], t.left[s][:]).then_inc(t.mid_ready, 1)

    def sums(s, k):
        act.wait_ge(t.summed, count(s, k, 0, ESLOTS))
        if has(s, k, ESLOTS, ESLOTS):
            act.wait_ge(t.added[s], 16 * G * k)
        nc.scalar.copy(t.sums[s][:].rearrange("p j d -> p (j d)"), bank[6 + s % 2][:, 0:G * D]).then_inc(t.sums_ready, 1)

    if layer == 0:
        parts = [(-3, mid), (-2, norms), (-3, sums)] + [(-1, found)] * near + [(-2, high)]
    else:
        parts = [(-3, sums), (-1, copy_ends), (-2, high), (-1, relu), (-2, mid)]
    rounds_of_blocks(act, parts, ESLOTS, GROUPS)


def edge_tensor(nc, pe, c, t, layer, near):
    bank = c["bank"]

    def bank_free(s, k):
        if has(s, k, 2, ESLOTS):
            pe.wait_ge(t.found_ready if layer == 0 else t.endsT_ready, count(s, k, 2, ESLOTS))

    def find(s, k):
        pe.wait_ge(t.onehot_ready, count(s, k, 0, ESLOTS))
        pe.wait_ge(t.window_in[s], 16 * G * (k + 1))
        bank_free(s, k)
        for j in range(G):
            for w in range(WK):
                window, onehot = t.window[s][:, j, w, :], t.onehot[s][:, j, w, :]
                if layer == 0:
                    last = nc.tensor.matmul(bank[s % 2][:, j * D:(j + 1) * D], onehot, window,
                                            start=w == 0, stop=w == WK - 1)
                else:
                    last = nc.tensor.matmul(bank[s % 2][0:D, j * P:(j + 1) * P], window, onehot,
                                            start=w == 0, stop=w == WK - 1)
        last.then_inc(t.found, 1)

    def turn(s, k):
        t.all_gathered(pe, s, k, near)
        if not near:
            bank_free(s, k)
        for j in range(G):
            if near:
                last = nc.tensor.matmul(bank[s % 2][D:2 * D, j * P:(j + 1) * P], t.ends[s][:, j, t.src_at, :],
                                        c["ident"][:], start=True, stop=True)
            else:
                last = nc.tensor.transpose(bank[s % 2][:, j * P:(j + 1) * P],
                                           t.ends[s][:, j].rearrange("p w d -> p (w d)"), c["ident"][:])
        last.then_inc(t.turned, 1)

    def hidden(s, k):
        pe.wait_ge(t.endsT_ready, count(s, k, 0, ESLOTS))
        if has(s, k, 2, ESLOTS):
            pe.wait_ge(t.hid_ready, count(s, k, 2, ESLOTS))
        nc.tensor.matmul(bank[2 + s % 2][:], c["mw1"][:], t.endsT[s][:], start=True,
                         stop=True).then_inc(t.hid_done, 1)

    def message(s, k):
        pe.wait_ge(t.hid_ready, count(s, k, 0, ESLOTS))
        if has(s, k, 2, ESLOTS):
            pe.wait_ge(t.msgs_ready, count(s, k, 2, ESLOTS))
        for j in range(G):
            last = nc.tensor.matmul(bank[4 + s % 2][:, j * D:(j + 1) * D], t.hid[s][:, j * P:(j + 1) * P],
                                    c["mw2"][:], start=True, stop=True)
        last.then_inc(t.mlp_done, 1)

    def sums(s, k):
        pe.wait_ge(t.same_ready, G * count(s, k, 0, ESLOTS))
        pe.wait_ge(t.high_ready, count(s, k, 0, ESLOTS))
        pe.wait_ge(t.mid_ready, count(s, k, 0, ESLOTS))
        pe.wait_ge(t.low_ready, count(s, k, 0, ESLOTS))
        if has(s, k, 2, ESLOTS):
            pe.wait_ge(t.sums_ready, count(s, k, 2, ESLOTS))
        for i in range(G):
            for j in range(i + 1):
                for part in range(3):
                    last = nc.tensor.matmul(bank[6 + s % 2][:, i * D:(i + 1) * D], t.same[s][:, same_block(j, i), :],
                                            t.parts[s][:, part, j, :], start=j == 0 and part == 0,
                                            stop=j == i and part == 2)
        last.then_inc(t.summed, 1)

    if layer == 0:
        parts = [(-3, sums)] + [(0, find)] * near
    else:
        parts = [(-3, sums)] + [(-1, find)] * near + [(-1, turn), (-2, message), (-1, hidden)]
    rounds_of_blocks(pe, parts, ESLOTS, GROUPS)


def node_phase2(nc, c, tabs, out):
    with ExitStack() as ctx:
        slots = Slots(nc, c, ctx, "n2")
        H = BLOCK // 2
        x1, res = slots.bufs("x1", [P, R, D]), slots.bufs("res", [P, R, D])
        hs = slots.bufs("hs", [P, R, 2, D])
        hsT, hid = slots.bufs("hsT", [P, BLOCK], 2), slots.bufs("hid", [P, BLOCK], 2)
        rows_in, stored = (slots.sems(n) for n in ("rows_in", "stored"))
        x1_biased, turned, low_ready, high_ready, hid_done, hid_ready, mlp_done, res_ready = (
            slots.sem(n) for n in ("x1_biased", "turned", "low_ready", "high_ready", "hid_done", "hid_ready",
                                   "mlp_done", "res_ready"))
        bank = c["bank"]
        hid_bank = [bank[2:4], bank[4:6]]
        block = ctx.enter_context(nc.Block())

        @block.sync
        def _(sp):
            def store(s, k):
                sp.wait_ge(res_ready, count(s, k))
                base = base_of(s, k)
                if base is LAST_BASE:
                    sp.wait_ge(stored[SLOTS - 1], 16 * k)
                sp.dma_start(rows_of(out, base), res[s][:].rearrange("p r d -> p (r d)")).then_inc(stored[s], 16)

            def load(s, k):
                if began(k):
                    sp.wait_ge(turned, count(s, k, SLOTS))
                    sp.wait_ge(res_ready, count(s, k, SLOTS))
                sp.dma_start(hs[s][:].rearrange("p r w d -> p (r w d)"),
                             rows_of(tabs["h1_agg"], 2 * base_of(s, k), 2 * R)).then_inc(rows_in[s], 16)
                sp.dma_start(x1[s][:].rearrange("p r d -> p (r d)"),
                             rows_of(tabs["x1"], base_of(s, k))).then_inc(rows_in[s], 16)

            rounds_of_blocks(sp, [(-SLOTS, store), (0, load)])
            for s in range(SLOTS):
                sp.wait_ge(stored[s], 16 * (ROUNDS + (s == 0)))

        @block.gpsimd
        def _(pool):
            def bias(s, k):
                pool.wait_ge(rows_in[s], 32 * (k + 1))
                nc.gpsimd.tensor_tensor(x1[s][:], x1[s][:], c["ub2_row"][:, :].unsqueeze(1).to_broadcast([P, R, D]),
                                        ALU.add).then_inc(x1_biased, 1)

            rounds_of_blocks(pool, [(0, bias)])

        def earlier(eng, sem, s, k, per=1):
            if has(s, k, 2):
                eng.wait_ge(sem, per * count(s, k, 2))

        @block.scalar
        def _(act):
            def low(s, k):
                act.wait_ge(turned, count(s, k))
                earlier(act, hid_done, s, k)
                nc.scalar.copy(hsT[s % 2][:, 0:H], bank[0][:]).then_inc(low_ready, 1)

            def relu(s, k):
                act.wait_ge(hid_done, count(s, k))
                earlier(act, mlp_done, s, k)
                for i in range(2):
                    nc.scalar.activation(hid[s % 2][:, i * H:(i + 1) * H], hid_bank[s % 2][i][:], ACT.Relu,
                                         bias=c["ub1_col"][:, 0:1]).then_inc(hid_ready, 1)

            rounds_of_blocks(act, [(0, low), (-1, relu)])

        @block.vector
        def _(dve):
            def high(s, k):
                dve.wait_ge(turned, count(s, k))
                earlier(dve, hid_done, s, k)
                nc.vector.tensor_copy(hsT[s % 2][:, H:2 * H], bank[1][:]).then_inc(high_ready, 1)

            def result(s, k):
                dve.wait_ge(mlp_done, count(s, k))
                dve.wait_ge(x1_biased, count(s, k))
                if began(k):
                    dve.wait_ge(stored[s], 16 * k)
                nc.vector.tensor_tensor(res[s][:], bank[6 + s % 2][:].rearrange("p (r d) -> p r d", d=D), x1[s][:],
                                        ALU.add).then_inc(res_ready, 1)

            rounds_of_blocks(dve, [(0, high), (-2, result)])

        @block.tensor
        def _(pe):
            def turn(s, k):
                pe.wait_ge(rows_in[s], 32 * (k + 1))
                if has(s, k, 1):
                    pe.wait_ge(low_ready, count(s, k, 1))
                    pe.wait_ge(high_ready, count(s, k, 1))
                for r in range(R):
                    last = nc.tensor.transpose(bank[r // 4][:, (r % 4) * P:(r % 4 + 1) * P],
                                               hs[s][:, r].rearrange("p w d -> p (w d)"), c["ident"][:])
                last.then_inc(turned, 1)

            def first(s, k):
                pe.wait_ge(low_ready, count(s, k))
                pe.wait_ge(high_ready, count(s, k))
                earlier(pe, hid_ready, s, k, 2)
                for i in range(2):
                    last = nc.tensor.matmul(hid_bank[s % 2][i][:], c["uw1"][:], hsT[s % 2][:, i * H:(i + 1) * H],
                                            start=True, stop=True)
                last.then_inc(hid_done, 1)

            def second(s, k):
                pe.wait_ge(hid_ready, 2 * count(s, k))
                earlier(pe, res_ready, s, k)
                for r in range(R):
                    last = nc.tensor.matmul(bank[6 + s % 2][:, r * D:(r + 1) * D], hid[s % 2][:, r * P:(r + 1) * P],
                                            c["uw2"][:], start=True, stop=True)
                last.then_inc(mlp_done, 1)

            rounds_of_blocks(pe, [(0, turn), (-1, first), (-2, second)])


_INS = ['x', 'src', 'dst', 'edge_weight', 'edge_weight_n2', 'L0_gnn_W', 'L0_gnn_b', 'L0_gnn_deg_coeff',
        'L0_gnn_coeff_param', 'L0_gnn_scale_param', 'L1_gnn_mW1', 'L1_gnn_mb1', 'L1_gnn_mW2', 'L1_gnn_mb2',
        'L1_gnn_uW1', 'L1_gnn_ub1', 'L1_gnn_uW2', 'L1_gnn_ub2']


def kernel(**inputs):
    import numpy as _np
    import concourse.bacc as _bacc
    from concourse import mybir as _mybir
    from concourse.bass_utils import run_bass_kernel_spmd as _run

    nc = _bacc.Bacc("TRN2", target_bir_lowering=False, num_devices=1)
    arrays, args = {}, []
    for name in _INS:
        a = _np.ascontiguousarray(inputs[name])
        arrays[f"in_{name}_dram"] = a
        args.append(nc.dram_tensor(f"in_{name}_dram", a.shape, _mybir.dt.from_np(a.dtype), kind="ExternalInput").ap())
    out = nc.dram_tensor("out_dram", (N, D), FP32, kind="ExternalOutput").ap()
    build(nc, *args, out)
    r = _run(nc, [arrays], core_ids=[0])
    return r.results[0]["out_dram"]
```

```python
import concourse.bass as bass
from concourse import mybir
from contextlib import ExitStack

FP32 = mybir.dt.float32
INT32 = mybir.dt.int32
BF16 = mybir.dt.bfloat16
ALU = mybir.AluOpType
ACT = mybir.ActivationFunctionType
AX = mybir.AxisListType

P = 128
N = 50000
E = 50000
D = 64
DH = 128
R = 8
BLOCK = P * R
BLOCKS = -(-N // BLOCK)
LAST_BASE = N - BLOCK
SLOTS = 8
ROUNDS = BLOCKS // SLOTS
G = 4
ESLOTS = 4
TILES = 392
GROUPS = TILES // G
WK = 3
WINDOW = P * WK
TRASH = N + P
ROWS = TRASH + G * P
SPARE = G + 1
CHUNKS = -(-TILES // P)
FULL = CHUNKS - 1
LAST_T = TILES - FULL * P
REST = E - FULL * P * P
REST_T, REST_E = REST // P, REST % P
EPS_LN = 1e-5
EPS_SIM = 1e-8

assert BLOCKS % SLOTS == 1 and SLOTS % 2 == 0 and GROUPS % 2 == 0 and TILES * P >= E and REST_E > 0


class Steps:

    def __init__(self, eng, sem, start=0):
        self.eng, self.sem, self.n, self.made = eng, sem, start, 0

    def mark(self, ins):
        self.n = self.n + 1
        self.made += 1
        ins.then_inc(self.sem, 1)

    def wait(self):
        self.eng.wait_ge(self.sem, self.n)

    def link(self, ins):
        self.mark(ins)
        self.wait()


class Semaphores:

    def __init__(self, nc):
        self.nc, self.ctx, self.made = nc, ExitStack(), []

    def new(self, name):
        self.made.append(self.ctx.enter_context(self.nc.semaphore(name)))
        return self.made[-1]

    def give_back(self):
        with self.nc.Block() as block:
            @block.sync
            def _(sp):
                for sem in self.made:
                    sp.sem_clear(sem)
        self.ctx.close()
        self.ctx, self.made = ExitStack(), []


def began(k):
    return not isinstance(k, int) or k > 0


def count(s, k, back=0, slots=0):
    return (slots or SLOTS) * k + s + 1 - back


def has(s, k, back, slots=0):
    return not isinstance(k, int) or count(s, k, back, slots) > 0


def rows_of(tab, base, r=R):
    return tab[bass.ds(base, P * r), :].rearrange("(p r) d -> p (r d)", r=r)


def build(nc, x, src, dst, edge_weight, edge_weight_n2, W, b, deg_coeff, coeff_param, scale_param,
          mW1, mb1, mW2, mb2, uW1, ub1, uW2, ub2, out):
    ctx = ExitStack()
    with ctx:
        def sb(name, shape, dt=FP32):
            return ctx.enter_context(nc.sbuf_tensor(name, shape, dt))

        def table(name, shape):
            return nc.dram_tensor(name, shape, FP32, kind="Internal").ap()

        tabs = {name: table(name, [ROWS, D]) for name in ("wh", "x1", "h1", "agg")}
        tabs["ends"] = table("ends", [2, TILES, P])

        c = dict(
            sems=Semaphores(nc),
            gathered=[[ctx.enter_context(nc.semaphore(f"e{layer}_gathered{s}")) for s in range(ESLOTS)]
                      for layer in range(2)],
            added=[[ctx.enter_context(nc.semaphore(f"e{layer}_added{s}")) for s in range(ESLOTS)]
                   for layer in range(2)],
            ident=sb("ident", [P, P]),
            not_before=sb("not_before", [P, G * P]),
            near=sb("near", [1, 1], INT32),
            first_i=sb("first_i", [1, TILES], INT32),
            first_f=sb("first_f", [P, GROUPS, G]),
            in_window=sb("in_window", [P, WK]),
            zeros=sb("zeros", [P, SPARE * D]),
            eps_ln=sb("eps_ln", [P, 1]),
            trash=sb("trash", [P, G]),
            w_blk=sb("w_blk", [P, 2 * D]),
            b_rows=sb("b_rows", [1, R, D]),
            ones_row=sb("ones_row", [1, P]),
            mw1=sb("mw1", [P, DH]), mb1_col=sb("mb1_col", [P, 1]),
            mw2=sb("mw2", [P, D]), mb2_row=sb("mb2_row", [P, D]),
            uw1=sb("uw1", [P, DH]), ub1_col=sb("ub1_col", [P, 1]),
            uw2=sb("uw2", [P, D]), ub2_row=sb("ub2_row", [P, D]),
            mix=sb("mix", [P, 3]),
            edge_f=sb("edge_f", [P, 3, GROUPS, G]),
            edge_i=sb("edge_i", [P, 2, GROUPS, G], INT32),
            bank=[ctx.enter_context(nc.psum_tensor(f"bank{i}", [P, 512], FP32)) for i in range(8)],
        )
        prepare(nc, c, tabs, src, dst, edge_weight, edge_weight_n2, W, b, deg_coeff, coeff_param,
                scale_param, mW1, mb1, mW2, mb2, uW1, ub1, uW2, ub2)
        node_phase0(nc, c, tabs, x)
        edge_phase(nc, c, tabs, layer=0)
        c["sems"].give_back()
        node_phase1(nc, c, tabs)
        edge_phase(nc, c, tabs, layer=1)
        node_phase2(nc, c, tabs, out)


def prepare(nc, c, tabs, src, dst, edge_weight, edge_weight_n2, W, b, deg_coeff, coeff_param,
            scale_param, mW1, mb1, mW2, mb2, uW1, ub1, uW2, ub2):
    with ExitStack() as ctx:
        def sb(name, shape, dt=FP32):
            return ctx.enter_context(nc.sbuf_tensor(name, shape, dt))

        def sem(name):
            return c["sems"].new(name)

        rows_i = sb("rows_i", [P, 2, CHUNKS, P], INT32)
        rows_f = sb("rows_f", [P, 4, CHUNKS, P])
        trash_i = sb("trash_i", [P, G], INT32)
        in_window_i = sb("in_window_i", [P, WK], INT32)
        least, greatest, first, short = (sb(n, [P, CHUNKS]) for n in ("least", "greatest", "first", "short"))
        below_n = sb("below_n", [P, CHUNKS, P])
        ones_col = sb("ones_col", [P, 1])
        first_row = sb("first_row", [1, TILES])
        shorts = sb("shorts", [1, 1])
        TC = GROUPS * G
        adj = sb("adj", [P, TC])
        deg = sb("deg", [P, TC + 1])
        soft = [sb(f"soft{i}", [P, TC + 1]) for i in range(3)]
        differ = sb("differ", [P, TC])
        dc = sb("dc", [P, 2])
        cp = sb("cp", [P, 3])
        cps = [sb(f"cps{i}", [P, 3]) for i in range(4)]

        pads_made, rows_loaded, consts_loaded, mlps_loaded = (
            sem("pads_made"), sem("rows_loaded"), sem("consts_loaded"), sem("mlps_loaded"))
        pool_steps, pool_made, dve_steps = sem("pool_steps"), sem("pool_made"), sem("dve_steps")
        rows_ready, cols_done, soft_in, soft_exp, mix_in, mix_exp = (
            sem("rows_ready"), sem("cols_done"), sem("soft_in"), sem("soft_exp"), sem("mix_in"),
            sem("mix_exp"))
        stats_clear, first_ready, first_done, first_row_ready, first_spread = (
            sem("stats_clear"), sem("first_ready"), sem("first_done"), sem("first_row_ready"), sem("first_spread"))
        soft_log, cols_taken, ends_stored, blk_clear = (
            sem("soft_log"), sem("cols_taken"), sem("ends_stored"), sem("blk_clear"))

        with nc.Block() as block:
            @block.sync
            def _(sp):
                sp.wait_ge(pads_made, 4)
                for i, (rows, arr) in enumerate(((rows_i[:, 0], src), (rows_i[:, 1], dst),
                                                 (rows_f[:, 2], edge_weight),
                                                 (rows_f[:, 3], edge_weight_n2))):
                    whole = FULL * P * P
                    sp.dma_start(rows[:, 0:FULL, :],
                                 arr[0:whole].rearrange("(c q e) -> q c e", q=P, e=P)).then_inc(rows_loaded, 16)
                    sp.dma_start(rows[0:REST_T, FULL, :],
                                 arr[whole:whole + REST_T * P].rearrange("(q e) -> q e", e=P)).then_inc(rows_loaded, 16)
                    sp.dma_start(rows[REST_T:REST_T + 1, FULL, 0:REST_E],
                                 arr[whole + REST_T * P:E].rearrange("(q e) -> q e", q=1)).then_inc(rows_loaded, 16)
                sp.wait_ge(rows_ready, 1)
                for i in range(2):
                    sp.dma_start(tabs["ends"][i, 0:FULL * P, :].rearrange("(c q) e -> q c e", q=P),
                                 rows_f[:, i, 0:FULL, :]).then_inc(ends_stored, 16)
                    sp.dma_start(tabs["ends"][i, FULL * P:TILES, :],
                                 rows_f[0:LAST_T, i, FULL, :]).then_inc(ends_stored, 16)
                sp.wait_ge(ends_stored, 64)

            @block.scalar
            def _(act):
                act.wait_ge(blk_clear, 1)
                row = lambda v: v.rearrange("(a n) -> a n", a=1)
                col = lambda v: v.rearrange("(n a) -> n a", a=1)
                consts = [(dc[:], row(deg_coeff).to_broadcast([P, 2])),
                          (cp[:], row(coeff_param).to_broadcast([P, 3])),
                          (deg[:, TC:TC + 1], row(scale_param).to_broadcast([P, 1])),
                          (c["w_blk"][0:D, 0:D], W), (c["w_blk"][D:2 * D, D:2 * D], W),
                          (c["b_rows"][:], row(b).unsqueeze(1).to_broadcast([1, R, D]))]
                mlps = [(c["mw1"][:], mW1), (c["mw2"][:], mW2), (c["uw1"][:], uW1), (c["uw2"][:], uW2),
                        (c["mb1_col"][:], col(mb1)), (c["ub1_col"][:], col(ub1)),
                        (c["mb2_row"][:], row(mb2).to_broadcast([P, D])),
                        (c["ub2_row"][:], row(ub2).to_broadcast([P, D]))]
                for to, of in consts:
                    act.dma_start(to, of).then_inc(consts_loaded, 16)
                act.wait_ge(rows_loaded, 12 * 16)
                with nc.allow_non_contiguous_dma(reason="bias columns"):
                    for to, of in mlps:
                        act.dma_start(to, of).then_inc(mlps_loaded, 16)
                act.wait_ge(soft_in, 1)
                nc.scalar.activation(soft[1][:], soft[2][:], ACT.Exp, scale=-1.0).then_inc(soft_exp, 1)
                act.wait_ge(mix_in, 1)
                nc.scalar.activation(cps[1][:], cps[0][:], ACT.Exp).then_inc(mix_exp, 1)
                act.wait_ge(soft_exp, 1)
                nc.scalar.activation(soft[2][:], soft[1][:], ACT.Ln, bias=1.0).then_inc(soft_log, 1)
                act.wait_ge(mlps_loaded, 8 * 16)

            @block.gpsimd
            def _(pool):
                steps = Steps(pool, pool_steps)
                for i in range(2):
                    nc.gpsimd.iota(rows_i[0:LAST_T, i, FULL, :], pattern=[[1, P]], base=N,
                                   channel_multiplier=0).then_inc(pads_made, 1)
                for i in range(2):
                    nc.gpsimd.memset(rows_f[0:LAST_T, 2 + i, FULL, :], 0.0).then_inc(pads_made, 1)
                nc.gpsimd.memset(c["w_blk"][:], 0.0).then_inc(blk_clear, 1)
                steps.mark(nc.gpsimd.memset(c["ident"][:], 0.0))
                steps.mark(nc.gpsimd.memset(c["not_before"][:], 1.0))
                for a, value in ((least, 0.0), (greatest, 0.0), (ones_col, 1.0)):
                    nc.gpsimd.memset(a[:], value).then_inc(stats_clear, 1)
                steps.mark(nc.gpsimd.iota(in_window_i[:], pattern=[[1, WK]], base=0, channel_multiplier=WK))
                steps.link(nc.gpsimd.iota(trash_i[:], pattern=[[P, G]], base=TRASH, channel_multiplier=1))
                nc.gpsimd.memset(c["ones_row"][:], 1.0).then_inc(pool_made, 1)
                nc.gpsimd.affine_select(out=c["ident"][:], in_=c["ident"][:], compare_op=ALU.not_equal,
                                        fill=1.0, base=0, pattern=[[-1, P]],
                                        channel_multiplier=1).then_inc(pool_made, 1)
                nc.gpsimd.affine_select(out=c["not_before"][:], in_=c["not_before"][:], compare_op=ALU.is_ge,
                                        fill=0.0, base=0, pattern=[[1, G * P]],
                                        channel_multiplier=-1).then_inc(pool_made, 1)
                nc.gpsimd.tensor_copy(c["trash"][:], trash_i[:]).then_inc(pool_made, 1)
                nc.gpsimd.tensor_copy(c["in_window"][:], in_window_i[:]).then_inc(pool_made, 1)
                nc.gpsimd.memset(c["zeros"][:], 0.0).then_inc(pool_made, 1)
                nc.gpsimd.memset(c["eps_ln"][:], EPS_LN).then_inc(pool_made, 1)

            @block.tensor
            def _(pe):
                pe.wait_ge(pool_made, 7)
                pe.wait_ge(rows_ready, 1)
                for i in range(4):
                    for ch in range(CHUNKS):
                        q = P if ch < FULL else LAST_T
                        last = nc.tensor.transpose(c["bank"][i][:, ch * P:ch * P + q],
                                                   rows_f[0:q, i, ch, :], c["ident"][0:q, 0:q])
                    last.then_inc(cols_done, 1)
                pe.wait_ge(first_ready, 1)
                pe.wait_ge(stats_clear, 3)
                for ch in range(CHUNKS):
                    q = P if ch < FULL else LAST_T
                    nc.tensor.transpose(c["bank"][4][0:1, ch * P:ch * P + q], first[0:q, ch:ch + 1],
                                        c["ident"][0:q, 0:q])
                nc.tensor.matmul(c["bank"][5][0:1, 0:CHUNKS], ones_col[:], short[:], start=True,
                                 stop=True).then_inc(first_done, 1)
                pe.wait_ge(first_row_ready, 1)
                nc.tensor.matmul(c["bank"][6][:, 0:TC], c["ones_row"][:], first_row[:], start=True,
                                 stop=True).then_inc(first_spread, 1)

            @block.vector
            def _(dve):
                steps = Steps(dve, dve_steps)
                dve.wait_ge(rows_loaded, 12 * 16)
                for i in range(2):
                    steps.mark(nc.vector.tensor_copy(rows_f[:, i, 0:FULL, :], rows_i[:, i, 0:FULL, :]))
                steps.mark(nc.vector.tensor_copy(rows_f[0:LAST_T, 0, FULL, :], rows_i[0:LAST_T, 0, FULL, :]))
                nc.vector.tensor_copy(rows_f[0:LAST_T, 1, FULL, :],
                                      rows_i[0:LAST_T, 1, FULL, :]).then_inc(rows_ready, 1)
                steps.wait()
                dve.wait_ge(rows_ready, 1)
                dve.wait_ge(stats_clear, 3)
                for q, ch in ((P, slice(0, FULL)), (LAST_T, slice(FULL, CHUNKS))):
                    steps.mark(nc.vector.tensor_reduce(least[0:q, ch], rows_f[0:q, 1, ch, :], AX.X, ALU.min))
                    steps.link(nc.vector.scalar_tensor_tensor(below_n[0:q, ch, :], rows_f[0:q, 1, ch, :], float(N),
                                                              rows_f[0:q, 1, ch, :], ALU.is_lt, ALU.mult))
                    steps.link(nc.vector.tensor_reduce(greatest[0:q, ch], below_n[0:q, ch, :], AX.X, ALU.max))
                steps.link(nc.vector.tensor_scalar(first[:], least[:], float(ROWS - WINDOW), None, ALU.min))
                steps.link(nc.vector.tensor_tensor(greatest[:], greatest[:], first[:], ALU.subtract))
                nc.vector.tensor_scalar(short[:], greatest[:], WINDOW - 0.5, None, ALU.is_gt).then_inc(first_ready, 1)
                dve.wait_ge(first_done, 1)
                nc.vector.tensor_copy(first_row[:], c["bank"][4][0:1, 0:TC]).then_inc(first_row_ready, 1)
                steps.mark(nc.vector.tensor_copy(c["first_i"][:], c["bank"][4][0:1, 0:TC]))
                steps.link(nc.vector.tensor_reduce(shorts[:], c["bank"][5][0:1, 0:CHUNKS], AX.X, ALU.add))
                steps.mark(nc.vector.tensor_scalar(c["near"][:], shorts[:], 0.5, None, ALU.is_lt))
                dve.wait_ge(first_spread, 1)
                steps.mark(nc.vector.tensor_copy(c["first_f"][:].rearrange("p g j -> p (g j)"), c["bank"][6][:, 0:TC]))
                dve.wait_ge(cols_done, 4)
                ef = c["edge_f"]
                flat = lambda a: a.rearrange("p g j -> p (g j)")
                for i in range(2):
                    steps.mark(nc.vector.tensor_copy(flat(ef[:, i, 0:GROUPS, :]), c["bank"][i][:, 0:TC]))
                    steps.mark(nc.vector.tensor_copy(flat(c["edge_i"][:, i, 0:GROUPS, :]), c["bank"][i][:, 0:TC]))
                steps.mark(nc.vector.tensor_copy(adj[:], c["bank"][2][:, 0:TC]))
                dve.wait_ge(consts_loaded, 6 * 16)
                steps.mark(nc.vector.tensor_scalar(soft[0][:, 0:TC], c["bank"][3][:, 0:TC], dc[:, 0:1], dc[:, 1:2],
                                                   ALU.mult, ALU.add))
                steps.link(nc.vector.tensor_copy(soft[0][:, TC:TC + 1], deg[:, TC:TC + 1]))
                nc.vector.scalar_tensor_tensor(soft[2][:], soft[0][:], -1.0, soft[0][:],
                                               ALU.mult, ALU.max).then_inc(soft_in, 1)
                steps.link(nc.vector.tensor_reduce(cps[3][:, 0:1], cp[:], AX.X, ALU.max))
                nc.vector.tensor_scalar(cps[0][:], cp[:], cps[3][:, 0:1], None, ALU.subtract).then_inc(mix_in, 1)
                steps.link(nc.vector.tensor_tensor(differ[:], flat(ef[:, 0, 0:GROUPS, :]),
                                                   flat(ef[:, 1, 0:GROUPS, :]), ALU.not_equal))
                steps.link(nc.vector.tensor_tensor(adj[:], adj[:], differ[:], ALU.mult))
                dve.wait_ge(mix_exp, 1)
                steps.link(nc.vector.tensor_reduce(cps[3][:, 1:2], cps[1][:], AX.X, ALU.add))
                steps.link(nc.vector.reciprocal(cps[3][:, 2:3], cps[3][:, 1:2]))
                steps.link(nc.vector.tensor_scalar(cps[2][:], cps[1][:], cps[3][:, 2:3], None, ALU.mult))
                dve.wait_ge(soft_log, 1)
                steps.link(nc.vector.scalar_tensor_tensor(soft[1][:], soft[0][:], 0.0, soft[2][:],
                                                          ALU.max, ALU.add))
                steps.mark(nc.vector.tensor_tensor(flat(ef[:, 2, 0:GROUPS, :]), adj[:], soft[1][:, 0:TC], ALU.mult))
                steps.link(nc.vector.tensor_scalar(c["mix"][:], cps[2][:], soft[1][:, TC:TC + 1], None, ALU.mult))


def rounds_of_blocks(eng, parts, slots=0, blocks=0):
    slots, blocks = slots or SLOTS, blocks or BLOCKS
    full = blocks // slots
    lag = -min(offset for offset, _ in parts)
    first = 1 + max(1, -(-lag // slots))

    def steps(k):
        for j in range(slots):
            for offset, part in parts:
                s, r = (j + offset) % slots, k + (j + offset) // slots
                if not isinstance(k, int) or 0 <= r * slots + s < blocks:
                    part(s, r)

    for k in range(first):
        steps(k)
    with eng.Fori(first, full) as k:
        steps(k)
    for k in range(full, full + first + 1):
        steps(k)


def base_of(s, k):
    if isinstance(k, int) and k * SLOTS + s == BLOCKS - 1:
        return LAST_BASE
    return (k * SLOTS + s) * BLOCK


def rows(a):
    return a.rearrange("p (r d) -> p r d", d=D)


def by_row(a):
    return a.unsqueeze(2).to_broadcast([P, R, D])


class Slots:

    def __init__(self, nc, c, ctx, tag):
        self.nc, self.ctx, self.tag, self.all = nc, ctx, tag, c["sems"]

    def bufs(self, name, shape, n=SLOTS, dt=FP32):
        return [self.ctx.enter_context(self.nc.sbuf_tensor(f"{self.tag}_{name}{s}", shape, dt)) for s in range(n)]

    def sem(self, name):
        return self.all.new(f"{self.tag}_{name}")

    def sems(self, name, n=SLOTS):
        return [self.sem(f"{name}{s}") for s in range(n)]


class LayerNorm:

    def __init__(self, nc, c, slots, h):
        self.nc, self.c, self.h = nc, c, h
        self.x, self.xc, self.sq = (slots.bufs(n, [P, R * D]) for n in ("x", "xc", "sq"))
        self.total, self.mean, self.ssq, self.std, self.rstd = (
            slots.bufs(n, [P, R]) for n in ("total", "mean", "ssq", "std", "rstd"))
        self.x_in = slots.sems("x_in")
        (self.total_ready, self.mean_ready, self.xc_ready, self.sq_ready, self.ssq_ready,
         self.std_ready, self.rstd_ready, self.h_ready) = (
            slots.sem(n) for n in ("total_ready", "mean_ready", "xc_ready", "sq_ready", "ssq_ready",
                                    "std_ready", "rstd_ready", "h_ready"))

    def dve_total(self, dve, s, k):
        dve.wait_ge(self.x_in[s], 16 * (k + 1))
        self.nc.vector.tensor_reduce(self.total[s][:], rows(self.x[s][:]), AX.X,
                                     ALU.add).then_inc(self.total_ready, 1)

    def dve_mean(self, dve, s, k):
        dve.wait_ge(self.total_ready, count(s, k))
        self.nc.vector.tensor_scalar(self.mean[s][:], self.total[s][:], 1.0 / D, None,
                                     ALU.mult).then_inc(self.mean_ready, 1)

    def pool_centre(self, pool, s, k):
        pool.wait_ge(self.mean_ready, count(s, k))
        if began(k):
            pool.wait_ge(self.h_ready, count(s, k, SLOTS))
        self.nc.gpsimd.tensor_tensor(rows(self.xc[s][:]), rows(self.x[s][:]), by_row(self.mean[s][:]),
                                     ALU.subtract).then_inc(self.xc_ready, 1)

    def act_square(self, act, s, k):
        act.wait_ge(self.xc_ready, count(s, k))
        if began(k):
            act.wait_ge(self.ssq_ready, count(s, k, SLOTS))
        self.nc.scalar.activation(self.sq[s][:], self.xc[s][:], ACT.Square).then_inc(self.sq_ready, 1)

    def dve_squares(self, dve, s, k):
        dve.wait_ge(self.sq_ready, count(s, k))
        self.nc.vector.tensor_reduce(self.ssq[s][:], rows(self.sq[s][:]), AX.X,
                                     ALU.add).then_inc(self.ssq_ready, 1)

    def act_std(self, act, s, k):
        act.wait_ge(self.ssq_ready, count(s, k))
        self.nc.scalar.activation(self.std[s][:], self.ssq[s][:], ACT.Sqrt, bias=self.c["eps_ln"][:, 0:1],
                                  scale=1.0 / D).then_inc(self.std_ready, 1)

    def dve_rstd(self, dve, s, k):
        dve.wait_ge(self.std_ready, count(s, k))
        self.nc.vector.reciprocal(self.rstd[s][:], self.std[s][:]).then_inc(self.rstd_ready, 1)

    def dve_h(self, dve, s, k):
        dve.wait_ge(self.rstd_ready, count(s, k))
        self.nc.vector.scalar_tensor_tensor(self.h[s], rows(self.xc[s][:]), 0.0, by_row(self.rstd[s][:]),
                                            ALU.max, ALU.mult).then_inc(self.h_ready, 1)


def node_phase0(nc, c, tabs, x):
    with ExitStack() as ctx:
        slots = Slots(nc, c, ctx, "n0")
        h, hT, wh, part, x1 = (slots.bufs(n, [P, R * D]) for n in ("h", "hT", "wh", "part", "x1"))
        ln = LayerNorm(nc, c, slots, [rows(a[:]) for a in h])
        stored = slots.sems("stored")
        turned, hT_ready, wh_done, wh_ready, x1_part, x1_ready = (
            slots.sem(n) for n in ("turned", "hT_ready", "wh_done", "wh_ready", "x1_part", "x1_ready"))
        pads_stored = slots.sem("pads_stored")
        turn_bank, wh_bank = c["bank"][0:2], c["bank"][2:4]
        block = ctx.enter_context(nc.Block())

        @block.sync
        def _(sp):
            for name in ("wh", "x1", "h1"):
                sp.dma_start(rows_of(tabs[name], N, SPARE), c["zeros"][:]).then_inc(pads_stored, 16)

            def store(s, k):
                sp.wait_ge(x1_ready, count(s, k))
                sp.wait_ge(wh_ready, count(s, k))
                base = base_of(s, k)
                if base is LAST_BASE:
                    sp.wait_ge(stored[SLOTS - 1], 32 * k)
                sp.dma_start(rows_of(tabs["wh"], base), wh[s][:]).then_inc(stored[s], 16)
                sp.dma_start(rows_of(tabs["x1"], base), x1[s][:]).then_inc(stored[s], 16)

            def load(s, k):
                if began(k):
                    sp.wait_ge(x1_ready, count(s, k, SLOTS))
                sp.dma_start(ln.x[s][:], rows_of(x, base_of(s, k))).then_inc(ln.x_in[s], 16)

            rounds_of_blocks(sp, [(-SLOTS, store), (0, load)])
            sp.wait_ge(pads_stored, 48)
            for s in range(SLOTS):
                sp.wait_ge(stored[s], 32 * (ROUNDS + (s == 0)))

        @block.vector
        def _(dve):
            def mean(s, k):
                ln.dve_total(dve, s, k)
                ln.dve_mean(dve, s, k)

            def squares(s, k):
                ln.dve_squares(dve, s, k)

            def normed(s, k):
                if began(k):
                    dve.wait_ge(turned, count(s, k, SLOTS))
                ln.dve_rstd(dve, s, k)
                ln.dve_h(dve, s, k)

            rounds_of_blocks(dve, [(-2, squares), (0, mean), (-2, normed)])

        @block.gpsimd
        def _(pool):
            def begin_x1(s, k):
                pool.wait_ge(wh_ready, count(s, k))
                pool.wait_ge(x1_part, count(s, k))
                if began(k):
                    pool.wait_ge(stored[s], 32 * k)
                nc.gpsimd.tensor_tensor(x1[s][:], part[s][:], ln.x[s][:], ALU.add).then_inc(x1_ready, 1)

            rounds_of_blocks(pool, [(-1, lambda s, k: ln.pool_centre(pool, s, k)), (-6, begin_x1)])

        @block.scalar
        def _(act):
            def copy_hT(s, k):
                act.wait_ge(turned, count(s, k))
                if began(k):
                    act.wait_ge(wh_done, count(s, k, SLOTS))
                nc.scalar.copy(hT[s][:], turn_bank[s % 2][:]).then_inc(hT_ready, 1)

            def copy_wh(s, k):
                act.wait_ge(wh_done, count(s, k))
                if began(k):
                    act.wait_ge(stored[s], 32 * k)
                nc.scalar.copy(wh[s][:], wh_bank[s % 2][:]).then_inc(wh_ready, 1)
                if began(k):
                    act.wait_ge(x1_ready, count(s, k, SLOTS))
                nc.scalar.activation(part[s][:], wh_bank[s % 2][:], ACT.Copy,
                                     scale=c["mix"][:, 2:3]).then_inc(x1_part, 1)

            rounds_of_blocks(act, [(-3, copy_hT), (-2, lambda s, k: ln.act_std(act, s, k)),
                                   (-1, lambda s, k: ln.act_square(act, s, k)), (-5, copy_wh)])

        @block.tensor
        def _(pe):
            def turn(s, k):
                pe.wait_ge(ln.h_ready, count(s, k))
                if has(s, k, 2):
                    pe.wait_ge(hT_ready, count(s, k, 2))
                for q in range(R // 2):
                    last = nc.tensor.transpose(turn_bank[s % 2][:, q * P:(q + 1) * P],
                                               h[s][:, q * 2 * D:(q + 1) * 2 * D], c["ident"][:])
                last.then_inc(turned, 1)

            def multiply(s, k):
                pe.wait_ge(hT_ready, count(s, k))
                if has(s, k, 2):
                    pe.wait_ge(wh_ready, count(s, k, 2))
                    pe.wait_ge(x1_part, count(s, k, 2))
                nc.tensor.matmul(wh_bank[s % 2][:], c["ones_row"][:], c["b_rows"][:].rearrange("p r d -> p (r d)"),
                                 start=True, stop=False)
                for q in range(R // 2):
                    last = nc.tensor.matmul(wh_bank[s % 2][:, q * P:(q + 1) * P], hT[s][:, q * P:(q + 1) * P],
                                            c["w_blk"][:], start=False, stop=q == R // 2 - 1)
                last.then_inc(wh_done, 1)

            rounds_of_blocks(pe, [(-3, turn), (-4, multiply)])


def node_phase1(nc, c, tabs):
    with ExitStack() as ctx:
        slots = Slots(nc, c, ctx, "n1")
        h = slots.bufs("h", [P, R * D])
        ln = LayerNorm(nc, c, slots, [rows(a[:]) for a in h])
        stored = slots.sems("stored")
        block = ctx.enter_context(nc.Block())

        @block.sync
        def _(sp):
            def store(s, k):
                sp.wait_ge(ln.h_ready, count(s, k))
                base = base_of(s, k)
                if base is LAST_BASE:
                    sp.wait_ge(stored[SLOTS - 1], 16 * k)
                sp.dma_start(rows_of(tabs["h1"], base), h[s][:]).then_inc(stored[s], 16)

            def load(s, k):
                if began(k):
                    sp.wait_ge(ln.xc_ready, count(s, k, SLOTS))
                sp.dma_start(ln.x[s][:], rows_of(tabs["x1"], base_of(s, k))).then_inc(ln.x_in[s], 16)

            rounds_of_blocks(sp, [(1 - SLOTS, store), (0, load)])
            for s in range(SLOTS):
                sp.wait_ge(stored[s], 16 * (ROUNDS + (s == 0)))

        @block.vector
        def _(dve):
            def normed(s, k):
                if began(k):
                    dve.wait_ge(stored[s], 16 * k)
                ln.dve_h(dve, s, k)

            rounds_of_blocks(dve, [(0, lambda s, k: ln.dve_total(dve, s, k)), (-3, lambda s, k: ln.dve_rstd(dve, s, k)),
                                   (0, lambda s, k: ln.dve_mean(dve, s, k)),
                                   (-2, lambda s, k: ln.dve_squares(dve, s, k)), (-3, normed)])

        @block.gpsimd
        def _(pool):
            rounds_of_blocks(pool, [(0, lambda s, k: ln.pool_centre(pool, s, k))])

        @block.scalar
        def _(act):
            rounds_of_blocks(act, [(-2, lambda s, k: ln.act_std(act, s, k)),
                                   (0, lambda s, k: ln.act_square(act, s, k))])


def edge_phase(nc, c, tabs, layer):
    with ExitStack() as ctx:
        slots = Slots(nc, c, ctx, f"e{layer}")
        t = EdgeBuffers(c, slots, layer)
        with nc.Block() as block:
            edge_programs(nc, block, c, tabs, t, layer)


def edge_programs(nc, block, c, tabs, t, layer):
    def both_ways(eng, program):
        near = eng.value_load(c["near"][0:1, 0:1], min_val=0, max_val=1)
        with eng.If(near > 0):
            program(True)
        with eng.Else():
            program(False)

    @block.sync
    def _(sp):
        both_ways(sp, lambda near: edge_loads(nc, sp, c, tabs, t, layer, near))

    @block.gpsimd
    def _(pool):
        both_ways(pool, lambda near: edge_pool(nc, pool, c, tabs, t, layer, near))

    @block.vector
    def _(dve):
        both_ways(dve, lambda near: edge_vector(nc, dve, c, t, layer, near))

    @block.scalar
    def _(act):
        both_ways(act, lambda near: edge_scalar(nc, act, c, t, layer, near))

    @block.tensor
    def _(pe):
        both_ways(pe, lambda near: edge_tensor(nc, pe, c, t, layer, near))


class EdgeBuffers:

    def __init__(self, c, slots, layer):
        def bufs(name, shape, dt=FP32):
            return slots.bufs(name, shape, ESLOTS, dt)

        self.src_at = layer
        self.dst_at = 1 - layer
        self.owners = bufs("owners", [P, G * P])
        self.targets = bufs("targets", [P, G * P]) if layer == 0 else self.owners
        self.window = bufs("window", [P, G, WK, D])
        self.window_row = bufs("window_row", [P, G, WK])
        self.onehot = bufs("onehot", [P, G, WK, P])
        self.ids = bufs("ids", [P, 2, G], INT32)
        self.ef = bufs("ef", [P, 3, G])
        self.ends = bufs("ends", [P, G, 2, D])
        self.same = bufs("same", [P, G * (G + 1) // 2, P], BF16)
        self.later = bufs("later", [P, G])
        self.trashed = bufs("trashed", [P, 2, G])
        self.to = bufs("to", [P, G], INT32)
        self.msgs, self.sums = bufs("msgs", [P, G, D]), bufs("sums", [P, G, D])
        self.parts, self.left = bufs("parts", [P, 3, G, D], BF16), bufs("left", [P, G, D])
        if layer == 0:
            self.prod, self.sq = bufs("prod", [P, G, D]), bufs("sq", [P, G, 2, D])
            self.dot, self.norm2, self.norm = bufs("dot", [P, G]), bufs("norm2", [P, G, 2]), bufs("norm", [P, G, 2])
            self.small = bufs("small", [P, 7, G])
        else:
            self.endsT, self.hid = bufs("endsT", [P, G * P]), bufs("hid", [P, G * P])
        self.numbers_in, self.window_in = (slots.sems(n, ESLOTS) for n in ("numbers_in", "window_in"))
        self.gathered, self.added = c["gathered"][layer], c["added"][layer]
        (self.onehot_ready, self.found, self.found_ready, self.same_ready, self.ids_ready, self.to_ready,
         self.msgs_ready, self.summed, self.sums_ready, self.steps, self.waited, self.row_ready,
         self.ef_ready, self.apart_ready, self.away_ready, self.zeroed,
         self.high_ready, self.left_ready, self.mid_ready, self.low_ready) = (
            slots.sem(n) for n in ("onehot_ready", "found", "found_ready", "same_ready", "ids_ready", "to_ready",
                                   "msgs_ready", "summed", "sums_ready", "steps", "waited", "row_ready",
                                   "ef_ready", "apart_ready", "away_ready", "zeroed",
                                   "high_ready", "left_ready", "mid_ready", "low_ready"))
        if layer == 0:
            self.norm2_ready, self.norm_ready = (
                slots.sem(n) for n in ("norm2_ready", "norm_ready"))
        else:
            self.turned, self.endsT_ready, self.hid_done, self.hid_ready, self.mlp_done = (
                slots.sem(n) for n in ("turned", "endsT_ready", "hid_done", "hid_ready", "mlp_done"))
        self.ends_used = self.msgs_ready if layer == 0 else self.turned

    def numbers(self, eng, s, k, near):
        eng.wait_ge(self.numbers_in[s], 16 * (2 if near and self.targets is not self.owners else 1) * (k + 1))

    def all_gathered(self, eng, s, k, near):
        eng.wait_ge(self.gathered[s], 16 * G * (1 if near else 2) * (k + 1))


def same_block(j, i):
    return j * G - j * (j - 1) // 2 + (i - j)


def edge_loads(nc, sp, c, tabs, t, layer, near):
    table = tabs["wh" if layer == 0 else "h1"]

    def numbers(s, k, end):
        return tabs["ends"][end, bass.ds((ESLOTS * k + s) * G, G), :].rearrange("t e -> (t e)").partition_broadcast(P)

    def load(s, k):
        if has(s, k, ESLOTS, ESLOTS):
            sp.wait_ge(t.same_ready, G * count(s, k, ESLOTS, ESLOTS))
            if near:
                sp.wait_ge(t.onehot_ready, count(s, k, ESLOTS, ESLOTS))
        sp.dma_start(t.owners[s][:], numbers(s, k, layer)).then_inc(t.numbers_in[s], 16)
        if not near:
            return
        if layer == 0:
            sp.dma_start(t.targets[s][:], numbers(s, k, 1)).then_inc(t.numbers_in[s], 16)
        if has(s, k, ESLOTS, ESLOTS):
            sp.wait_ge(t.found, count(s, k, ESLOTS, ESLOTS))
        for j in range(G):
            first = sp.value_load(c["first_i"][0:1, bass.ds((ESLOTS * k + s) * G + j, 1)], min_val=0,
                                  max_val=ROWS - WINDOW)
            sp.dma_start(t.window[s][:, j].rearrange("p w d -> p (w d)"),
                         rows_of(table, first, WK)).then_inc(t.window_in[s], 16)

    def clear(s, k):
        sp.dma_start(rows_of(tabs["agg"], (ESLOTS * k + s) * G * P, G), c["zeros"][:, 0:G * D]).then_inc(t.zeroed, 16)

    if layer == 0:
        sp.dma_start(rows_of(tabs["agg"], ROWS - SPARE * P, SPARE), c["zeros"][:]).then_inc(t.zeroed, 16)
        sp.wait_ge(t.zeroed, 16)
    rounds_of_blocks(sp, [(0, load)] + [(0, clear)] * (layer == 0), ESLOTS, GROUPS)
    if layer == 0:
        sp.wait_ge(t.zeroed, 16 * (1 + GROUPS))


def edge_pool(nc, pool, c, tabs, t, layer, near):
    gathered_tab, added_tab = (tabs["wh"], tabs["x1"]) if layer == 0 else (tabs["h1"], tabs["agg"])

    def gather(s, k):
        pool.wait_ge(t.ids_ready, count(s, k, 0, ESLOTS))
        if has(s, k, ESLOTS, ESLOTS):
            pool.wait_ge(t.ends_used, count(s, k, ESLOTS, ESLOTS))
        pool.sem_inc(t.waited, 1)
        for j in range(G):
            for end, at in ((0, t.src_at), (1, t.dst_at))[:1 if near else 2]:
                pool.indirect_dma_start(
                    out=t.ends[s][:, j, at, :], out_offset=None, in_=gathered_tab,
                    in_offset=bass.IndirectOffsetOnAxis(ap=t.ids[s][:, end, j:j + 1], axis=0),
                ).then_inc(t.gathered[s], 16)

    def scatter(s, k):
        pool.wait_ge(t.to_ready, count(s, k, 0, ESLOTS))
        pool.wait_ge(t.sums_ready, count(s, k, 0, ESLOTS))
        if s:
            pool.wait_ge(t.added[s - 1], 16 * G * (k + 1))
        elif began(k):
            pool.wait_ge(t.added[ESLOTS - 1], 16 * G * k)
        pool.sem_inc(t.waited, 1)
        for j in range(G):
            pool.indirect_dma_start(
                out=added_tab, out_offset=bass.IndirectOffsetOnAxis(ap=t.to[s][:, j:j + 1], axis=0),
                in_=t.sums[s][:, j, :], in_offset=None, compute_op=ALU.add).then_inc(t.added[s], 16)

    rounds_of_blocks(pool, [(0, gather), (-3, scatter)], ESLOTS, GROUPS)
    for s in range(ESLOTS):
        pool.wait_ge(t.added[s], 16 * G * -(-(GROUPS - s) // ESLOTS))


def edge_vector(nc, dve, c, t, layer, near):
    dot_steps, weigh_steps = G, 8

    def of_group(a, s, k):
        return a[:, :, bass.ds(ESLOTS * k + s, 1), :].rearrange("p w a j -> p w (a j)")

    def ahead(s, k):
        if has(s, k, ESLOTS, ESLOTS):
            t.all_gathered(dve, s, k - 1, near)
        nc.vector.tensor_copy(t.ids[s][:], of_group(c["edge_i"], s, k)).then_inc(t.ids_ready, 1)
        if not near:
            return
        group = c["first_f"][:, bass.ds(ESLOTS * k + s, 1), :].rearrange("p a j -> p (a j)")
        nc.vector.tensor_tensor(
            t.window_row[s][:], group.unsqueeze(2).to_broadcast([P, G, WK]),
            c["in_window"][:, :].unsqueeze(1).to_broadcast([P, G, WK]), ALU.add).then_inc(t.row_ready, 1)
        dve.wait_ge(t.row_ready, count(s, k, 0, ESLOTS))
        t.numbers(dve, s, k, near)
        if has(s, k, ESLOTS, ESLOTS):
            dve.wait_ge(t.found, count(s, k, ESLOTS, ESLOTS))
        nc.vector.tensor_tensor(
            t.onehot[s][:], t.targets[s][:].rearrange("p (j e) -> p j e", e=P).unsqueeze(2).to_broadcast([P, G, WK, P]),
            t.window_row[s][:].unsqueeze(3).to_broadcast([P, G, WK, P]), ALU.is_equal).then_inc(t.onehot_ready, 1)

    def match(s, k):
        if has(s, k, ESLOTS, ESLOTS):
            dve.wait_ge(t.to_ready, count(s, k, ESLOTS, ESLOTS))
        nc.vector.tensor_copy(t.ef[s][:], of_group(c["edge_f"], s, k)).then_inc(t.ef_ready, 1)
        owner = t.ef[s][:, layer, :]
        dve.wait_ge(t.ef_ready, count(s, k, 0, ESLOTS))
        t.numbers(dve, s, k, near)
        if has(s, k, ESLOTS, ESLOTS):
            dve.wait_ge(t.summed, count(s, k, ESLOTS, ESLOTS))
        for j in range(G):
            n = (G - j) * P
            nc.vector.scalar_tensor_tensor(
                t.same[s][:, same_block(j, j):same_block(j, G - 1) + 1, :].rearrange("p b i -> p (b i)"),
                t.owners[s][:, j * P:], owner[:, j:j + 1], c["not_before"][:, 0:n],
                ALU.is_equal, ALU.mult, accum_out=t.later[s][:, j:j + 1]).then_inc(t.same_ready, 1)
        nc.vector.tensor_tensor(t.trashed[s][:, 0, :], c["trash"][:], owner, ALU.subtract).then_inc(t.apart_ready, 1)

    def own_steps(s, k, before):
        return Steps(dve, t.steps, (dot_steps + weigh_steps) * (count(s, k, 0, ESLOTS) - 1) + before)

    def compare(s, k):
        steps = own_steps(s, k, 0)
        t.all_gathered(dve, s, k, near)
        if near:
            dve.wait_ge(t.found_ready, count(s, k, 0, ESLOTS))
        for j in range(G):
            steps.mark(nc.vector.scalar_tensor_tensor(
                t.prod[s][:, j], t.ends[s][:, j, 0, :], 1.0, t.ends[s][:, j, 1, :], ALU.mult, ALU.mult,
                accum_out=t.dot[s][:, j:j + 1]))
        assert steps.made == dot_steps

    def weigh(s, k):
        steps = own_steps(s, k, dot_steps)
        a = t.small[s]
        dve.wait_ge(t.norm_ready, count(s, k, 0, ESLOTS))
        steps.link(nc.vector.tensor_tensor(a[:, 0, :], t.norm[s][:, :, 0], t.norm[s][:, :, 1], ALU.mult))
        steps.link(nc.vector.tensor_scalar(a[:, 1, :], a[:, 0, :], EPS_SIM, None, ALU.max))
        steps.link(nc.vector.reciprocal(a[:, 2, :], a[:, 1, :]))
        steps.link(nc.vector.tensor_tensor(a[:, 3, :], t.dot[s][:], a[:, 2, :], ALU.mult))
        steps.mark(nc.vector.tensor_scalar(a[:, 4, :], a[:, 3, :], 0.0, c["mix"][:, 0:1], ALU.max, ALU.mult))
        steps.link(nc.vector.tensor_scalar(a[:, 5, :], a[:, 3, :], 0.0, c["mix"][:, 1:2], ALU.min, ALU.mult))
        steps.link(nc.vector.tensor_tensor(a[:, 6, :], a[:, 4, :], a[:, 5, :], ALU.add))
        steps.link(nc.vector.tensor_tensor(a[:, 0, :], a[:, 6, :], t.ef[s][:, 2, :], ALU.mult))
        nc.vector.tensor_tensor(t.msgs[s][:], t.ends[s][:, :, 1, :], a[:, 0, :].unsqueeze(2).to_broadcast([P, G, D]),
                                ALU.mult).then_inc(t.msgs_ready, 1)
        assert steps.made == weigh_steps

    def bias(s, k):
        dve.wait_ge(t.mlp_done, count(s, k, 0, ESLOTS))
        nc.vector.tensor_tensor(t.msgs[s][:], c["bank"][4 + s % 2][:, 0:G * D].rearrange("p (j d) -> p j d", d=D),
                                c["mb2_row"][:, :].unsqueeze(1).to_broadcast([P, G, D]),
                                ALU.add).then_inc(t.msgs_ready, 1)

    def leave(s, k):
        dve.wait_ge(t.high_ready, count(s, k, 0, ESLOTS))
        nc.vector.tensor_tensor(t.left[s][:], t.msgs[s][:], t.parts[s][:, 0], ALU.subtract).then_inc(t.left_ready, 1)

    def low(s, k):
        dve.wait_ge(t.mid_ready, count(s, k, 0, ESLOTS))
        nc.vector.tensor_tensor(t.parts[s][:, 2], t.left[s][:], t.parts[s][:, 1], ALU.subtract).then_inc(t.low_ready, 1)

    def address(s, k):
        owner = t.ef[s][:, layer, :]
        dve.wait_ge(t.same_ready, G * count(s, k, 0, ESLOTS))
        dve.wait_ge(t.apart_ready, count(s, k, 0, ESLOTS))
        nc.vector.scalar_tensor_tensor(t.trashed[s][:, 1, :], t.later[s][:], 1.5, t.trashed[s][:, 0, :],
                                       ALU.is_gt, ALU.mult).then_inc(t.away_ready, 1)
        dve.wait_ge(t.away_ready, count(s, k, 0, ESLOTS))
        if has(s, k, ESLOTS, ESLOTS):
            dve.wait_ge(t.added[s], 16 * G * k)
        nc.vector.tensor_tensor(t.to[s][:], t.trashed[s][:, 1, :], owner, ALU.add).then_inc(t.to_ready, 1)

    if layer == 0:
        parts = [(-3, leave), (0, ahead), (-3, low), (-1, match), (-2, compare), (-2, address), (-2, weigh)]
    else:
        parts = [(-3, low), (0, ahead), (-1, match), (-2, address), (-2, bias), (-2, leave)]
    rounds_of_blocks(dve, parts, ESLOTS, GROUPS)


def edge_scalar(nc, act, c, t, layer, near):
    bank = c["bank"]

    def found(s, k):
        act.wait_ge(t.found, count(s, k, 0, ESLOTS))
        if has(s, k, ESLOTS, ESLOTS):
            act.wait_ge(t.ends_used, count(s, k, ESLOTS, ESLOTS))
        nc.scalar.copy(t.ends[s][:, :, t.dst_at, :],
                       bank[s % 2][:, 0:G * D].rearrange("p (j d) -> p j d", d=D)).then_inc(t.found_ready, 1)

    def norms(s, k):
        t.all_gathered(act, s, k, near)
        if near:
            act.wait_ge(t.found_ready, count(s, k, 0, ESLOTS))
        if has(s, k, ESLOTS, ESLOTS):
            act.wait_ge(t.msgs_ready, count(s, k, ESLOTS, ESLOTS))
        for j in range(G):
            for end in range(2):
                nc.scalar.activation(t.sq[s][:, j, end, :], t.ends[s][:, j, end, :], ACT.Square,
                                     accum_out=t.norm2[s][:, j, end:end + 1]).then_inc(t.norm2_ready, 1)
        act.wait_ge(t.norm2_ready, 2 * G * count(s, k, 0, ESLOTS))
        nc.scalar.activation(t.norm[s][:], t.norm2[s][:], ACT.Sqrt).then_inc(t.norm_ready, 1)

    def copy_ends(s, k):
        act.wait_ge(t.turned, count(s, k, 0, ESLOTS))
        nc.scalar.copy(t.endsT[s][:], bank[s % 2][:]).then_inc(t.endsT_ready, 1)

    def relu(s, k):
        act.wait_ge(t.hid_done, count(s, k, 0, ESLOTS))
        nc.scalar.activation(t.hid[s][:], bank[2 + s % 2][:], ACT.Relu,
                             bias=c["mb1_col"][:, 0:1]).then_inc(t.hid_ready, 1)

    def high(s, k):
        act.wait_ge(t.msgs_ready, count(s, k, 0, ESLOTS))
        if has(s, k, ESLOTS, ESLOTS):
            act.wait_ge(t.summed, count(s, k, ESLOTS, ESLOTS))
        nc.scalar.copy(t.parts[s][:, 0], t.msgs[s][:]).then_inc(t.high_ready, 1)

    def mid(s, k):
        act.wait_ge(t.left_ready, count(s, k, 0, ESLOTS))
        nc.scalar.copy(t.parts[s][:, 1], t.left[s][:]).then_inc(t.mid_ready, 1)

    def sums(s, k):
        act.wait_ge(t.summed, count(s, k, 0, ESLOTS))
        if has(s, k, ESLOTS, ESLOTS):
            act.wait_ge(t.added[s], 16 * G * k)
        nc.scalar.copy(t.sums[s][:].rearrange("p j d -> p (j d)"),
                       bank[6 + s % 2][:, 0:G * D]).then_inc(t.sums_ready, 1)

    if layer == 0:
        parts = [(-3, mid), (-2, norms), (-3, sums)] + [(-1, found)] * near + [(-2, high)]
    else:
        parts = [(-3, sums), (-1, copy_ends), (-2, high), (-1, relu), (-2, mid)]
    rounds_of_blocks(act, parts, ESLOTS, GROUPS)


def edge_tensor(nc, pe, c, t, layer, near):
    bank = c["bank"]

    def bank_free(s, k):
        if has(s, k, 2, ESLOTS):
            pe.wait_ge(t.found_ready if layer == 0 else t.endsT_ready, count(s, k, 2, ESLOTS))

    def find(s, k):
        pe.wait_ge(t.onehot_ready, count(s, k, 0, ESLOTS))
        pe.wait_ge(t.window_in[s], 16 * G * (k + 1))
        bank_free(s, k)
        for j in range(G):
            for w in range(WK):
                window, onehot = t.window[s][:, j, w, :], t.onehot[s][:, j, w, :]
                if layer == 0:
                    last = nc.tensor.matmul(bank[s % 2][:, j * D:(j + 1) * D], onehot, window,
                                            start=w == 0, stop=w == WK - 1)
                else:
                    last = nc.tensor.matmul(bank[s % 2][0:D, j * P:(j + 1) * P], window, onehot,
                                            start=w == 0, stop=w == WK - 1)
        last.then_inc(t.found, 1)

    def turn(s, k):
        t.all_gathered(pe, s, k, near)
        if not near:
            bank_free(s, k)
        for j in range(G):
            if near:
                last = nc.tensor.matmul(bank[s % 2][D:2 * D, j * P:(j + 1) * P], t.ends[s][:, j, t.src_at, :],
                                        c["ident"][:], start=True, stop=True)
            else:
                last = nc.tensor.transpose(bank[s % 2][:, j * P:(j + 1) * P],
                                           t.ends[s][:, j].rearrange("p w d -> p (w d)"), c["ident"][:])
        last.then_inc(t.turned, 1)

    def hidden(s, k):
        pe.wait_ge(t.endsT_ready, count(s, k, 0, ESLOTS))
        if has(s, k, 2, ESLOTS):
            pe.wait_ge(t.hid_ready, count(s, k, 2, ESLOTS))
        nc.tensor.matmul(bank[2 + s % 2][:], c["mw1"][:], t.endsT[s][:], start=True,
                         stop=True).then_inc(t.hid_done, 1)

    def message(s, k):
        pe.wait_ge(t.hid_ready, count(s, k, 0, ESLOTS))
        if has(s, k, 2, ESLOTS):
            pe.wait_ge(t.msgs_ready, count(s, k, 2, ESLOTS))
        for j in range(G):
            last = nc.tensor.matmul(bank[4 + s % 2][:, j * D:(j + 1) * D], t.hid[s][:, j * P:(j + 1) * P],
                                    c["mw2"][:], start=True, stop=True)
        last.then_inc(t.mlp_done, 1)

    def sums(s, k):
        pe.wait_ge(t.same_ready, G * count(s, k, 0, ESLOTS))
        pe.wait_ge(t.high_ready, count(s, k, 0, ESLOTS))
        pe.wait_ge(t.mid_ready, count(s, k, 0, ESLOTS))
        pe.wait_ge(t.low_ready, count(s, k, 0, ESLOTS))
        if has(s, k, 2, ESLOTS):
            pe.wait_ge(t.sums_ready, count(s, k, 2, ESLOTS))
        for i in range(G):
            for j in range(i + 1):
                for part in range(3):
                    last = nc.tensor.matmul(bank[6 + s % 2][:, i * D:(i + 1) * D], t.same[s][:, same_block(j, i), :],
                                            t.parts[s][:, part, j, :], start=j == 0 and part == 0,
                                            stop=j == i and part == 2)
        last.then_inc(t.summed, 1)

    if layer == 0:
        parts = [(-3, sums)] + [(0, find)] * near
    else:
        parts = [(-3, sums)] + [(-1, find)] * near + [(-1, turn), (-2, message), (-1, hidden)]
    rounds_of_blocks(pe, parts, ESLOTS, GROUPS)


def node_phase2(nc, c, tabs, out):
    with ExitStack() as ctx:
        slots = Slots(nc, c, ctx, "n2")
        H = BLOCK // 2
        x1, res = slots.bufs("x1", [P, R, D]), slots.bufs("res", [P, R, D])
        parts = slots.bufs("parts", [P, 2, R, D])
        hs = slots.bufs("hs", [P, R, 2, D])
        hsT, hid = slots.bufs("hsT", [P, BLOCK], 2), slots.bufs("hid", [P, BLOCK], 2)
        rows_in, stored = (slots.sems(n) for n in ("rows_in", "stored"))
        beside_ready, x1_biased, turned, low_ready, high_ready, hid_done, hid_ready, mlp_done, res_ready = (
            slots.sem(n) for n in ("beside_ready", "x1_biased", "turned", "low_ready", "high_ready", "hid_done",
                                   "hid_ready", "mlp_done", "res_ready"))
        bank = c["bank"]
        hid_bank = [bank[2:4], bank[4:6]]
        block = ctx.enter_context(nc.Block())

        @block.sync
        def _(sp):
            def store(s, k):
                sp.wait_ge(res_ready, count(s, k))
                base = base_of(s, k)
                if base is LAST_BASE:
                    sp.wait_ge(stored[SLOTS - 1], 16 * k)
                sp.dma_start(rows_of(out, base), res[s][:].rearrange("p r d -> p (r d)")).then_inc(stored[s], 16)

            def load(s, k):
                if began(k):
                    sp.wait_ge(beside_ready, count(s, k, SLOTS))
                    sp.wait_ge(res_ready, count(s, k, SLOTS))
                for i, name in enumerate(("h1", "agg")):
                    sp.dma_start(parts[s][:, i].rearrange("p r d -> p (r d)"),
                                 rows_of(tabs[name], base_of(s, k))).then_inc(rows_in[s], 16)
                sp.dma_start(x1[s][:].rearrange("p r d -> p (r d)"),
                             rows_of(tabs["x1"], base_of(s, k))).then_inc(rows_in[s], 16)

            rounds_of_blocks(sp, [(-SLOTS, store), (0, load)])
            for s in range(SLOTS):
                sp.wait_ge(stored[s], 16 * (ROUNDS + (s == 0)))

        @block.gpsimd
        def _(pool):
            def bias(s, k):
                pool.wait_ge(rows_in[s], 48 * (k + 1))
                nc.gpsimd.tensor_tensor(x1[s][:], x1[s][:], c["ub2_row"][:, :].unsqueeze(1).to_broadcast([P, R, D]),
                                        ALU.add).then_inc(x1_biased, 1)

            rounds_of_blocks(pool, [(0, bias)])

        def earlier(eng, sem, s, k, per=1):
            if has(s, k, 2):
                eng.wait_ge(sem, per * count(s, k, 2))

        @block.scalar
        def _(act):
            def low(s, k):
                act.wait_ge(turned, count(s, k))
                earlier(act, hid_done, s, k)
                nc.scalar.copy(hsT[s % 2][:, 0:H], bank[0][:]).then_inc(low_ready, 1)

            def relu(s, k):
                act.wait_ge(hid_done, count(s, k))
                earlier(act, mlp_done, s, k)
                for i in range(2):
                    nc.scalar.activation(hid[s % 2][:, i * H:(i + 1) * H], hid_bank[s % 2][i][:], ACT.Relu,
                                         bias=c["ub1_col"][:, 0:1]).then_inc(hid_ready, 1)

            rounds_of_blocks(act, [(-1, low), (-2, relu)])

        @block.vector
        def _(dve):
            def beside(s, k):
                dve.wait_ge(rows_in[s], 48 * (k + 1))
                if began(k):
                    dve.wait_ge(turned, count(s, k, SLOTS))
                nc.vector.tensor_copy(hs[s][:], parts[s][:].rearrange("p w r d -> p r w d")).then_inc(beside_ready, 1)

            def high(s, k):
                dve.wait_ge(turned, count(s, k))
                earlier(dve, hid_done, s, k)
                nc.vector.tensor_copy(hsT[s % 2][:, H:2 * H], bank[1][:]).then_inc(high_ready, 1)

            def result(s, k):
                dve.wait_ge(mlp_done, count(s, k))
                dve.wait_ge(x1_biased, count(s, k))
                if began(k):
                    dve.wait_ge(stored[s], 16 * k)
                nc.vector.tensor_tensor(res[s][:], bank[6 + s % 2][:].rearrange("p (r d) -> p r d", d=D), x1[s][:],
                                        ALU.add).then_inc(res_ready, 1)

            rounds_of_blocks(dve, [(-1, high), (0, beside), (-3, result)])

        @block.tensor
        def _(pe):
            def turn(s, k):
                pe.wait_ge(beside_ready, count(s, k))
                if has(s, k, 1):
                    pe.wait_ge(low_ready, count(s, k, 1))
                    pe.wait_ge(high_ready, count(s, k, 1))
                for r in range(R):
                    last = nc.tensor.transpose(bank[r // 4][:, (r % 4) * P:(r % 4 + 1) * P],
                                               hs[s][:, r].rearrange("p w d -> p (w d)"), c["ident"][:])
                last.then_inc(turned, 1)

            def first(s, k):
                pe.wait_ge(low_ready, count(s, k))
                pe.wait_ge(high_ready, count(s, k))
                earlier(pe, hid_ready, s, k, 2)
                for i in range(2):
                    last = nc.tensor.matmul(hid_bank[s % 2][i][:], c["uw1"][:], hsT[s % 2][:, i * H:(i + 1) * H],
                                            start=True, stop=True)
                last.then_inc(hid_done, 1)

            def second(s, k):
                pe.wait_ge(hid_ready, 2 * count(s, k))
                earlier(pe, res_ready, s, k)
                for r in range(R):
                    last = nc.tensor.matmul(bank[6 + s % 2][:, r * D:(r + 1) * D], hid[s % 2][:, r * P:(r + 1) * P],
                                            c["uw2"][:], start=True, stop=True)
                last.then_inc(mlp_done, 1)

            rounds_of_blocks(pe, [(-1, turn), (-2, first), (-3, second)])


_INS = ['x', 'src', 'dst', 'edge_weight', 'edge_weight_n2', 'L0_gnn_W', 'L0_gnn_b', 'L0_gnn_deg_coeff',
        'L0_gnn_coeff_param', 'L0_gnn_scale_param', 'L1_gnn_mW1', 'L1_gnn_mb1', 'L1_gnn_mW2', 'L1_gnn_mb2',
        'L1_gnn_uW1', 'L1_gnn_ub1', 'L1_gnn_uW2', 'L1_gnn_ub2']


def kernel(**inputs):
    import numpy as _np
    import concourse.bacc as _bacc
    from concourse import mybir as _mybir
    from concourse.bass_utils import run_bass_kernel_spmd as _run

    nc = _bacc.Bacc("TRN2", target_bir_lowering=False, num_devices=1)
    arrays, args = {}, []
    for name in _INS:
        a = _np.ascontiguousarray(inputs[name])
        arrays[f"in_{name}_dram"] = a
        args.append(nc.dram_tensor(f"in_{name}_dram", a.shape, _mybir.dt.from_np(a.dtype), kind="ExternalInput").ap())
    out = nc.dram_tensor("out_dram", (N, D), FP32, kind="ExternalOutput").ap()
    build(nc, *args, out)
    r = _run(nc, [arrays], core_ids=[0])
    return r.results[0]["out_dram"]
```
